# Optimizing a Trainium2 kernel written in Bass

```python
import numpy as np
import jax
import jax.numpy as jnp

def _softmax(x, axis=-1):
    return jax.nn.softmax(x, axis=axis)

def _gelu(x):
    return jax.nn.gelu(x, approximate=True)

def _silu(x):
    return jax.nn.silu(x)

def _sigmoid(x):
    return jax.nn.sigmoid(x)

def _layernorm(x, axis=-1, eps=1e-05):
    m = jnp.mean(x, axis=axis, keepdims=True)
    v = jnp.var(x, axis=axis, keepdims=True)
    return (x - m) / jnp.sqrt(v + eps)

def _scatter_add(tgt, idx, src, axis=0):
    return tgt.at[idx].add(src)

def _segment_sum(src, seg, n):
    return jax.ops.segment_sum(src, seg, n)
kernel_name = 'mk_audio_tower_d1_tok_audfeat2048_r4_eb7997'

def setup_inputs(seed: int=0):
    np.random.seed(seed)
    _w = jnp.asarray

    def _rec_inputs():
        import jax
        import jax.numpy as jnp
        _rk = jax.random.key(seed)
        x = 7.22013e-05 + 1.00017 * jax.random.normal(jax.random.fold_in(_rk, 1), (64, 256, 64), jnp.float32)
        return x
    x = _rec_inputs()

    def _L0_tok_setup():
        import jax, jax.numpy as jnp
        import numpy as np
        from jax import lax
        B, T, CC, CI, CO, K, L = (32, 256, 64, 64, 80, 5, 4)
        EPS = 1e-05

        def _conv1d(x, w, b, pad):
            y = lax.conv_general_dilated(x, w, window_strides=(1,), padding=((pad, pad),), dimension_numbers=('NCH', 'OIH', 'NCH'))
            return y + b[None, :, None]
        key = jax.random.key(seed)
        ks = jax.random.split(key, 12)
        s = 0.05
        return {'enc_output': jax.random.normal(ks[0], (B, T, CC), jnp.float32), 'up_w': jax.random.normal(ks[1], (CC, CI, 2), jnp.float32) * s, 'up_b': jax.random.normal(ks[2], (CI,), jnp.float32) * s, 'bn_gamma': jnp.ones((CI,), jnp.float32), 'bn_beta': jnp.zeros((CI,), jnp.float32), 'bn_mean': jax.random.normal(ks[3], (CI,), jnp.float32) * 0.1, 'bn_var': jax.random.uniform(ks[4], (CI,), jnp.float32) + 0.5, 'conv_ws': jax.random.normal(ks[5], (L, 2 * CI, CI, K), jnp.float32) * s, 'conv_bs': jax.random.normal(ks[6], (L, 2 * CI), jnp.float32) * s, 'cond_ws': jax.random.normal(ks[7], (L, CI, CC), jnp.float32) * s, 'cond_bs': jax.random.normal(ks[8], (L, CI), jnp.float32) * s, 'out_w': jax.random.normal(ks[9], (CO, CI), jnp.float32) * s, 'out_b': jax.random.normal(ks[10], (CO,), jnp.float32) * s}
    _L0_tok_all = _L0_tok_setup()
    _L0_tok_in = {k: v for k, v in _L0_tok_all.items() if k in ('up_w', 'up_b', 'bn_gamma', 'bn_beta', 'bn_mean', 'bn_var', 'conv_ws', 'conv_bs', 'cond_ws', 'cond_bs', 'out_w', 'out_b')}
    del _L0_tok_all

    def _L0_attn_setup():
        import jax, jax.numpy as jnp
        import numpy as np
        import math
        D = 512
        K = 64
        NUM_HEADS = 32
        HEAD_DIM = K // NUM_HEADS
        SPARSITY = 0.1
        LN_EPS = 1e-05
        key = jax.random.key(seed)
        ks = jax.random.split(key, 12)
        B, S = (1, 256)
        sc = 0.02
        inp = {'x': jax.random.normal(ks[0], (B, S, D), dtype=jnp.float32), 'gamma': jnp.ones((D,), jnp.float32), 'beta': jnp.zeros((D,), jnp.float32), 'W1': jax.random.normal(ks[1], (128, D), jnp.float32) * sc, 'b1': jnp.zeros((128,), jnp.float32), 'W2': jax.random.normal(ks[2], (64, 128), jnp.float32) * sc, 'b2': jnp.zeros((64,), jnp.float32), 'W3': jax.random.normal(ks[3], (1, 64), jnp.float32) * sc, 'b3': jnp.zeros((1,), jnp.float32), 'Wqkv': jax.random.normal(ks[4], (3 * K, D), jnp.float32) * sc, 'bqkv': jnp.zeros((3 * K,), jnp.float32), 'Wout': jax.random.normal(ks[5], (D, K), jnp.float32) * sc, 'bout': jnp.zeros((D,), jnp.float32)}
        return inp
    _L0_attn_all = _L0_attn_setup()
    _L0_attn_in = {k: v for k, v in _L0_attn_all.items() if k in ('gamma', 'beta', 'W1', 'b1', 'W2', 'b2', 'W3', 'b3', 'Wqkv', 'bqkv', 'Wout', 'bout')}
    del _L0_attn_all

    def _L0_ffn_setup():
        import jax, jax.numpy as jnp
        import numpy as np
        E = 8
        K = 2
        B, L, D = (2, 512, 512)
        I = 192
        IS = 1024
        key = jax.random.key(seed)
        ks = jax.random.split(key, 8)
        s = 0.02
        return {'hidden_states': jax.random.normal(ks[0], (B, L, D), jnp.float32), 'gate_w': jax.random.normal(ks[1], (E, D), jnp.float32) * s, 'gate_up_proj': jax.random.normal(ks[2], (E, 2 * I, D), jnp.float32) * s, 'down_proj': jax.random.normal(ks[3], (E, D, I), jnp.float32) * s, 'shared_gate_w': jax.random.normal(ks[4], (IS, D), jnp.float32) * s, 'shared_up_w': jax.random.normal(ks[5], (IS, D), jnp.float32) * s, 'shared_down_w': jax.random.normal(ks[6], (D, IS), jnp.float32) * s, 'shared_expert_gate_w': jax.random.normal(ks[7], (1, D), jnp.float32) * s}
    _L0_ffn_all = _L0_ffn_setup()
    _L0_ffn_in = {k: v for k, v in _L0_ffn_all.items() if k in ('gate_w', 'gate_up_proj', 'down_proj', 'shared_gate_w', 'shared_up_w', 'shared_down_w', 'shared_expert_gate_w')}
    del _L0_ffn_all
    return {'x': x, 'L0_tok_up_w': _L0_tok_in['up_w'], 'L0_tok_up_b': _L0_tok_in['up_b'], 'L0_tok_bn_gamma': _L0_tok_in['bn_gamma'], 'L0_tok_bn_beta': _L0_tok_in['bn_beta'], 'L0_tok_bn_mean': _L0_tok_in['bn_mean'], 'L0_tok_bn_var': _L0_tok_in['bn_var'], 'L0_tok_conv_ws': _L0_tok_in['conv_ws'], 'L0_tok_conv_bs': _L0_tok_in['conv_bs'], 'L0_tok_cond_ws': _L0_tok_in['cond_ws'], 'L0_tok_cond_bs': _L0_tok_in['cond_bs'], 'L0_tok_out_w': _L0_tok_in['out_w'], 'L0_tok_out_b': _L0_tok_in['out_b'], 'L0_attn_gamma': _L0_attn_in['gamma'], 'L0_attn_beta': _L0_attn_in['beta'], 'L0_attn_W1': _L0_attn_in['W1'], 'L0_attn_b1': _L0_attn_in['b1'], 'L0_attn_W2': _L0_attn_in['W2'], 'L0_attn_b2': _L0_attn_in['b2'], 'L0_attn_W3': _L0_attn_in['W3'], 'L0_attn_b3': _L0_attn_in['b3'], 'L0_attn_Wqkv': _L0_attn_in['Wqkv'], 'L0_attn_bqkv': _L0_attn_in['bqkv'], 'L0_attn_Wout': _L0_attn_in['Wout'], 'L0_attn_bout': _L0_attn_in['bout'], 'L0_ffn_gate_w': _L0_ffn_in['gate_w'], 'L0_ffn_gate_up_proj': _L0_ffn_in['gate_up_proj'], 'L0_ffn_down_proj': _L0_ffn_in['down_proj'], 'L0_ffn_shared_gate_w': _L0_ffn_in['shared_gate_w'], 'L0_ffn_shared_up_w': _L0_ffn_in['shared_up_w'], 'L0_ffn_shared_down_w': _L0_ffn_in['shared_down_w'], 'L0_ffn_shared_expert_gate_w': _L0_ffn_in['shared_expert_gate_w']}

def reference(x, L0_tok_up_w, L0_tok_up_b, L0_tok_bn_gamma, L0_tok_bn_beta, L0_tok_bn_mean, L0_tok_bn_var, L0_tok_conv_ws, L0_tok_conv_bs, L0_tok_cond_ws, L0_tok_cond_bs, L0_tok_out_w, L0_tok_out_b, L0_attn_gamma, L0_attn_beta, L0_attn_W1, L0_attn_b1, L0_attn_W2, L0_attn_b2, L0_attn_W3, L0_attn_b3, L0_attn_Wqkv, L0_attn_bqkv, L0_attn_Wout, L0_attn_bout, L0_ffn_gate_w, L0_ffn_gate_up_proj, L0_ffn_down_proj, L0_ffn_shared_gate_w, L0_ffn_shared_up_w, L0_ffn_shared_down_w, L0_ffn_shared_expert_gate_w):
    import jax
    import jax.numpy as jnp

    def _L0_tok_ref(enc_output, up_w, up_b, bn_gamma, bn_beta, bn_mean, bn_var, conv_ws, conv_bs, cond_ws, cond_bs, out_w, out_b):
        import jax, jax.numpy as jnp
        import numpy as np
        from jax import lax
        B, T, CC, CI, CO, K, L = (32, 256, 64, 64, 80, 5, 4)
        EPS = 1e-05

        def _conv1d(x, w, b, pad):
            y = lax.conv_general_dilated(x, w, window_strides=(1,), padding=((pad, pad),), dimension_numbers=('NCH', 'OIH', 'NCH'))
            return y + b[None, :, None]
        enc = jnp.transpose(enc_output, (0, 2, 1))
        wt = jnp.flip(up_w, axis=-1).transpose(1, 0, 2)
        x = lax.conv_general_dilated(enc, wt, window_strides=(1,), padding=((1, 1),), lhs_dilation=(2,), dimension_numbers=('NCH', 'OIH', 'NCH'))
        x = x + up_b[None, :, None]
        x = (x - bn_mean[None, :, None]) * (bn_gamma / jnp.sqrt(bn_var + EPS))[None, :, None] + bn_beta[None, :, None]
        x = jax.nn.relu(x)
        enc_rep = jnp.repeat(enc, 2, axis=-1)
        pad = (K - 1) // 2
        for l in range(L):
            res = x
            y = _conv1d(x, conv_ws[l], conv_bs[l], pad)
            y1, y2 = (y[:, :CI], y[:, CI:])
            c = jnp.einsum('oc,bct->bot', cond_ws[l], enc_rep) + cond_bs[l][None, :, None]
            c = jax.nn.soft_sign(c)
            x = jax.nn.sigmoid(y1) * (y2 + c) + res
        out = jnp.einsum('oc,bct->bot', out_w, x) + out_b[None, :, None]
        return out

    def _L0_attn_ref(x, gamma, beta, W1, b1, W2, b2, W3, b3, Wqkv, bqkv, Wout, bout):
        import jax, jax.numpy as jnp
        import numpy as np
        import math
        D = 512
        K = 64
        NUM_HEADS = 32
        HEAD_DIM = K // NUM_HEADS
        SPARSITY = 0.1
        LN_EPS = 1e-05
        B, S, d = x.shape
        mu = jnp.mean(x, -1, keepdims=True)
        var = jnp.var(x, -1, keepdims=True)
        xn = (x - mu) * jax.lax.rsqrt(var + LN_EPS) * gamma + beta
        h = jnp.einsum('bsd,fd->bsf', xn, W1)
        pair = jax.nn.relu(h[:, :, None, :] - h[:, None, :, :] + b1)
        pair = jax.nn.relu(jnp.einsum('bijf,gf->bijg', pair, W2) + b2)
        sim = jnp.einsum('bijg,og->bijo', pair, W3)[..., 0] + b3[0]
        diag = jnp.arange(S)
        sim = sim.at[:, diag, diag].set(0.0)
        k_sparse = max(1, int(S * SPARSITY))
        _, top_idx = jax.lax.top_k(sim, k_sparse)
        mask = jnp.full((B, S, S), -jnp.inf, dtype=x.dtype)
        bidx = jnp.arange(B)[:, None, None]
        iidx = jnp.arange(S)[None, :, None]
        mask = mask.at[bidx, iidx, top_idx].set(0.0)
        qkv = jnp.einsum('bsd,ed->bse', xn, Wqkv) + bqkv
        q, k, v = jnp.split(qkv, 3, axis=-1)

        def heads(t):
            return t.reshape(B, S, NUM_HEADS, HEAD_DIM).transpose(0, 2, 1, 3)
        q, k, v = (heads(q), heads(k), heads(v))
        scores = jnp.einsum('bhid,bhjd->bhij', q, k) / math.sqrt(HEAD_DIM)
        scores = scores + mask[:, None, :, :]
        attn = jax.nn.softmax(scores, axis=-1)
        ao = jnp.einsum('bhij,bhjd->bhid', attn, v)
        ao = ao.transpose(0, 2, 1, 3).reshape(B, S, K)
        out = jnp.einsum('bsk,dk->bsd', ao, Wout) + bout
        return x + out

    def _L0_ffn_ref(hidden_states, gate_w, gate_up_proj, down_proj, shared_gate_w, shared_up_w, shared_down_w, shared_expert_gate_w):
        import jax, jax.numpy as jnp
        import numpy as np
        E = 8
        K = 2
        B, L, D = (2, 512, 512)
        I = 192
        IS = 1024
        Bb, Ll, Dd = hidden_states.shape
        h = hidden_states.reshape(-1, Dd)
        silu = jax.nn.silu
        shared = silu(h @ shared_gate_w.T) * (h @ shared_up_w.T) @ shared_down_w.T
        shared_out = jax.nn.sigmoid(h @ shared_expert_gate_w.T) * shared
        logits = h @ gate_w.T
        probs = jax.nn.softmax(logits, axis=-1)
        topk_w, topk_idx = jax.lax.top_k(probs, K)
        topk_w = topk_w / jnp.sum(topk_w, axis=-1, keepdims=True)
        cw = jnp.sum(jax.nn.one_hot(topk_idx, E, dtype=h.dtype) * topk_w[..., None], axis=1)
        gu = jnp.einsum('td,efd->tef', h, gate_up_proj)
        g, u = jnp.split(gu, 2, axis=-1)
        act = silu(g) * u
        out = jnp.einsum('tei,edi->ted', act, down_proj)
        partial = jnp.einsum('ted,te->td', out, cw)
        return (partial + shared_out).reshape(Bb, Ll, Dd)
    h = _L0_tok_ref(x, L0_tok_up_w, L0_tok_up_b, L0_tok_bn_gamma, L0_tok_bn_beta, L0_tok_bn_mean, L0_tok_bn_var, L0_tok_conv_ws, L0_tok_conv_bs, L0_tok_cond_ws, L0_tok_cond_bs, L0_tok_out_w, L0_tok_out_b)
    h = h + _L0_attn_ref(_layernorm(h, axis=-1), L0_attn_gamma, L0_attn_beta, L0_attn_W1, L0_attn_b1, L0_attn_W2, L0_attn_b2, L0_attn_W3, L0_attn_b3, L0_attn_Wqkv, L0_attn_bqkv, L0_attn_Wout, L0_attn_bout)
    h = h + _L0_ffn_ref(_layernorm(h, axis=-1), L0_ffn_gate_w, L0_ffn_gate_up_proj, L0_ffn_down_proj, L0_ffn_shared_gate_w, L0_ffn_shared_up_w, L0_ffn_shared_down_w, L0_ffn_shared_expert_gate_w)
    return h

_drawn_inputs = setup_inputs


def setup_inputs(seed=0):
    import zlib

    import numpy as np

    out = dict(_drawn_inputs(seed))
    spreads = {'L0_tok_bn_gamma': (1.0, 0.2),
     'L0_tok_bn_beta': (0.0, 0.1),
     'L0_attn_gamma': (1.0, 0.6),
     'L0_attn_beta': (0.0, 0.8),
     'L0_attn_b1': (0.0, 0.726),
     'L0_attn_b2': (0.0, 0.373),
     'L0_attn_bqkv': (0.0, 0.69),
     'L0_attn_bout': (0.0, 0.1)}
    factors = {'L0_ffn_gate_w': 3.698,
     'L0_ffn_gate_up_proj': 3.205,
     'L0_ffn_down_proj': 3.206,
     'L0_ffn_shared_expert_gate_w': 68.899}
    for name, (base, spread) in spreads.items():
        noise = np.random.default_rng([zlib.crc32(name.encode()), seed]).standard_normal(out[name].shape)
        drawn = base * np.exp(spread * noise) if base else spread * noise
        out[name] = jnp.asarray(drawn.astype(out[name].dtype))
    for name, factor in factors.items():
        out[name] = (out[name] * factor).astype(out[name].dtype)
    return out
```

```python
import concourse.bass as bass
from concourse import mybir
from contextlib import ExitStack

F32 = mybir.dt.float32
U32 = mybir.dt.uint32
ALU = mybir.AluOpType
ACT = mybir.ActivationFunctionType
AX = mybir.AxisListType

BN_EPS = 1e-5
LN_EPS = 1e-5
TOPK = 8


def at_least(eng, sem, value):
    if isinstance(value, int) and value <= 0:
        return
    eng.wait_ge(sem, value)


def tokens_and_attention(nc, t):
    B, CC, T = t["xT"].shape[0] - 1, *t["xT"].shape[1:]
    L, S = 4, t["out_wT"].shape[1]
    D = 2 * T
    KD = D // 128
    HF = t["W1T"].shape[1]
    PG = t["W2T"].shape[1]
    KQ = t["WoutT"].shape[0]
    HD = 2
    NH = KQ // HD
    PAD = D + 4
    CH = 10
    NCH = S // CH
    HALF = S // 2
    CW = CH * HALF

    with ExitStack() as ctx:
        def sb(name, shape, dt=F32):
            return ctx.enter_context(nc.sbuf_tensor(name, shape, dt))

        def ps(name, shape):
            return ctx.enter_context(nc.psum_tensor(name, shape, F32))

        def sem(name):
            return ctx.enter_context(nc.semaphore(name))

        up_w = sb("up_w", [CC, 2, 2 * CC])
        bn = sb("bn", [128, 6])
        up_scale = sb("up_scale", [128, 1])
        up_shift = sb("up_shift", [128, 1])
        conv_w = sb("conv_w", [128, L, 3, 128])
        gate_b = sb("gate_b", [64, L])
        lin_b = sb("lin_b", [128, 2])
        cond_w = sb("cond_w", [CC + 1, L * CC])
        tok_w = sb("tok_w", [CC, S])
        tok_b = sb("tok_b", [S, 1])
        gamma = sb("gamma", [128, KD])
        beta = sb("beta", [128, KD])
        w1 = sb("w1", [128, KD, HF])
        b1 = sb("b1", [128, 1])
        w2 = sb("w2", [128, PG])
        b2 = sb("b2", [128, 1])
        w3 = sb("w3", [128, 23])
        b3 = sb("b3", [16, 1])
        wqkv = sb("wqkv", [128, KD, 3 * KQ])
        bqkv = sb("bqkv", [S, 3 * KQ])
        wout = sb("wout", [KQ + 1, D])
        ident = sb("ident", [128, 128])
        key_no = sb("key_no", [S, 1])
        off_diag = sb("off_diag", [S, S])
        minus_half = sb("minus_half", [128, 1])

        enc = sb("enc", [CC + 1, 2, T])
        xs = sb("xs", [128, PAD])
        cabs = sb("cabs", [128, 2 * T])
        cond = sb("cond", [128, 2, T])
        th = sb("th", [128, D])
        lin = sb("lin", [128, D])
        gated = sb("gated", [128, D])
        h = sb("h", [S, D])
        xa = sb("xa", [S, D])
        hx = sb("hx", [S, 2, D])
        xn = sb("xn", [S, D])
        stats = sb("stats", [S, 2, 6])
        mv = sb("mv", [S, 2, 2])
        veps = sb("veps", [S, 2])
        rstd = sb("rstd", [S, 2])
        xnT = sb("xnT", [128, KD, S])
        hp = sb("hp", [128, S])
        hm = sb("hm", [128, S])
        pair = sb("pair", [128, 4, CH, S])
        r2 = sb("r2", [128, 2, CW])
        sim16 = sb("sim16", [16, CW])
        qkv = sb("qkv", [S, 2, 3 * KQ])
        sim_in = sb("sim_in", [S, S])
        sim = sb("sim", [S, S])
        top = sb("top", [S, TOPK])
        idx = sb("idx", [S, TOPK], U32)
        idx_all = sb("idx_all", [S, S, TOPK], U32)
        pick = sb("pick", [S, TOPK, S])
        prod = sb("prod", [S, TOPK, KQ])
        score = sb("score", [S, TOPK, NH])
        smax = sb("smax", [S, NH])
        prob = sb("prob", [S, TOPK, NH])
        psum_ = sb("psum_", [S, NH])
        pinv = sb("pinv", [S, NH])
        pv = sb("pv", [S, TOPK, KQ])
        ao = sb("ao", [S, KQ])
        aon = sb("aon", [S, 128])
        aoT = sb("aoT", [KQ + 1, S])
        h1 = sb("h1", [S, D])

        Y = ps("Y", [128, 512])
        C = ps("C", [128, 512])
        Z = [ps("Z0", [128, 512]), ps("Z1", [128, 512])]
        W = ps("W", [128, 512])
        G = ps("G", [128, 2, 512])
        X = ps("X", [128, 512])

        sim_d = nc.dram_tensor("sim_d", (16, CW), F32, kind="Internal").ap()
        idx_d = nc.dram_tensor("idx_d", (S, TOPK), U32, kind="Internal").ap()

        w_in = sem("weights_in")
        consts = sem("consts")
        zeros_set = sem("zeros_set")
        const_chain = sem("const_chain")
        bn_ready = sem("bn_ready")
        enc_in = [sem("enc_in0"), sem("enc_in1")]
        up_done, cond_done, conv_done, tok_done = sem("up_done"), sem("cond_done"), sem("conv_done"), sem("tok_done")
        x_top, x_bot = sem("x_top"), sem("x_bot")
        abs_done, soft_done = sem("abs_done"), sem("soft_done")
        th_done, lin_done, gated_done = sem("th_done"), sem("lin_done"), sem("gated_done")
        h_done, ln_chain, veps_done, rstd_done = sem("h_done"), sem("ln_chain"), sem("veps_done"), sem("rstd_done")
        xn_done, hx_done = sem("xn_done"), sem("hx_done")
        xnT_psum, xnT_done, hT_psum, hpm_done = sem("xnT_psum"), sem("xnT_done"), sem("hT_psum"), sem("hpm_done")
        qkv_psum, qkv_done = sem("qkv_psum"), sem("qkv_done")
        pair_done, z_done, r2_done, w3_done = sem("pair_done"), sem("z_done"), sem("r2_done"), sem("w3_done")
        sim16_done, sim_out, sim_back, sim_done = sem("sim16_done"), sem("sim_out"), sem("sim_back"), sem("sim_done")
        top_done, idx_done, idx_out, idx_back = sem("top_done"), sem("idx_done"), sem("idx_out"), sem("idx_back")
        pick_done, g_done = sem("pick_done"), sem("g_done")
        at_chain, exp_in, exp_done, ao_done = sem("at_chain"), sem("exp_in"), sem("exp_done"), sem("ao_done")
        aoT_psum, aoT_done, wo_done = sem("aoT_psum"), sem("aoT_done"), sem("wo_done")
        h1_done = sem("h1_done")
        h1_out = sem("h1_out")

        block = ctx.enter_context(nc.Block())

        def schedule(eng, step):
            step(0, 0, True, False, False)
            step(0, 1, True, True, False)
            with eng.Fori(1, B // 2) as n:
                step(n, 0, True, True, True)
                step(n, 1, True, True, True)
            step(B // 2, 0, False, True, True)
            step(B // 2, 1, False, False, True)

        @block.sync
        def _(sp):
            loads = [
                (up_w[:, :, 0:CC], t["up_wT"]), (up_w[:, :, CC:], t["up_wT"]),
                (conv_w[0:CC, :, 0, :], t["convT"][0]), (conv_w[CC:, :, 0, :], t["convT"][1]),
                (conv_w[0:CC, :, 1, :], t["convT"][2]), (conv_w[CC:, :, 1, :], t["convT"][3]),
                (conv_w[0:CC, :, 2, :], t["convT"][4]),
                (lin_b[:, :], t["lin_b"]), (cond_w[0:CC, :], t["condT"]), (cond_w[CC:CC + 1, :], t["cond_b"]),
                (tok_w[:, :], t["out_wT"]), (tok_b[:, :], t["out_b"]), (gate_b[:, :], t["gate_b"]),
                (gamma[:, :], t["gamma"]),
                (beta[:, :], t["beta"]),
                (w1[:, :, :], t["W1T"].rearrange("(k p) f -> p k f", p=128)),
                (b1[:, :], t["b1"]), (w2[:, :], t["W2T"]),
                (b2[0:PG, :], t["b2"]), (b2[PG:, :], t["b2"]),
                (w3[0:PG, 7:8], t["W3T"]), (w3[PG:, 15:16], t["W3T"]),
                (b3[:, :], t["b3"].partition_broadcast(16)),
                (wqkv[:, :, :], t["WqkvT"].rearrange("(k p) f -> p k f", p=128)),
                (bqkv[:, :], t["bqkv"].partition_broadcast(S)),
                (wout[0:KQ, :], t["WoutT"]), (wout[KQ:KQ + 1, :], t["bout"]),
            ]
            for i, name in enumerate(["up_b", "bn_gamma", "bn_beta", "bn_mean", "bn_var"]):
                loads += [(bn[0:CC, i:i + 1], t[name]), (bn[CC:, i:i + 1], t[name])]
            sp.wait_ge(zeros_set, 1)
            sp.dma_start(enc[0:CC, 0, :], t["xT"][0]).then_inc(enc_in[0], 16)
            for dst, src in loads:
                sp.dma_start(dst, src).then_inc(w_in, 16)

            def step(n, o, tok, prs, att):
                b = 2 * n + o
                if tok:
                    last = 0
                    at_least(sp, cond_done, b)
                    if isinstance(n, int):
                        src = t["xT"][b + 1]
                    else:
                        src = t["xT"][bass.ds(b + 1, 1)].squeeze(0)
                    sp.dma_start(enc[0:CC, (o + 1) % 2, :], src).then_inc(enc_in[(o + 1) % 2], 16)
                if att:
                    a = b - 2
                    sp.wait_ge(idx_done, a + 1)
                    sp.dma_start(idx_d, idx[:, :]).then_inc(idx_out, 16)
                    sp.wait_ge(idx_out, 16 * a + 16)
                    sp.dma_start(idx_all[:, :, :], idx_d.partition_broadcast(S)).then_inc(idx_back, 16)
                if att:
                    a = b - 2
                    sp.wait_ge(h1_done, a + 1)
                    if isinstance(n, int):
                        dst = t["h1"][a]
                    else:
                        dst = t["h1"][bass.ds(a, 1)].squeeze(0)
                    sp.dma_start(dst, h1[:, :]).then_inc(h1_out, 16)
                if prs:
                    p = b - 1
                    sp.wait_ge(sim16_done, p + 1)
                    sp.dma_start(sim_d, sim16[:, :]).then_inc(sim_out, 16)
                    if att:
                        sp.wait_ge(h1_out, 16 * a + 16)
                    sp.wait_ge(sim_out, 16 * p + 16)
                    at_least(sp, sim_done, p)
                    sp.dma_start(sim_in[:, :].rearrange("i (m j) -> i m j", m=2),
                                 sim_d.rearrange("(m c) (i j) -> (c i) m j", m=2, i=CH)).then_inc(sim_back, 16)
            schedule(sp, step)
            sp.wait_ge(h1_out, 16 * B)

        @block.gpsimd
        def _(pool):
            pool.iota(key_no[:, :], [[1, 1]], base=0, channel_multiplier=1,
                      allow_small_or_imprecise_dtypes=True).then_inc(consts, 1)
            pool.wait_ge(zeros_set, 1)
            pool.wait_ge(consts, 1)
            pool.affine_select(out=ident[:, :], in_=ident[:, :], compare_op=ALU.not_equal, fill=1.0,
                               base=0, pattern=[[-1, 128]], channel_multiplier=1).then_inc(consts, 1)
            pool.affine_select(out=off_diag[:, :], in_=off_diag[:, :], compare_op=ALU.not_equal, fill=0.0,
                               base=0, pattern=[[-1, S]], channel_multiplier=1).then_inc(consts, 1)
            pool.wait_ge(consts, 3)
            pool.wait_ge(w_in, 16 * 37)
            pool.tensor_scalar(bn[:, 5:6], bn[:, 4:5], BN_EPS, None, ALU.add).then_inc(const_chain, 1)
            pool.wait_ge(const_chain, 1)
            pool.tensor_tensor(bn[:, 5:6], bn[:, 5:6], minus_half[:, :], ALU.pow).then_inc(const_chain, 1)

            def step(n, o, tok, prs, att):
                b = 2 * n + o
                if att:
                    a = b - 2
                    pool.wait_ge(sim_back, 16 * a + 16)
                    at_least(pool, idx_done, a)
                    pool.tensor_tensor(sim[:, :], sim_in[:, :], off_diag[:, :], ALU.mult).then_inc(sim_done, 1)
                if tok:
                    for k in range(2):
                        pool.wait_ge(veps_done, 2 * b + k + 1)
                        pool.tensor_tensor(rstd[:, k:k + 1], veps[:, k:k + 1], minus_half[0:S, :],
                                           ALU.pow).then_inc(rstd_done, 1)
            schedule(pool, step)

        @block.tensor
        def _(pe):
            pe.wait_ge(consts, 3)
            pe.wait_ge(w_in, 16 * 37)

            def conv(l):
                for m in range(3):
                    mm = pe.matmul(Y[:, 0:D], conv_w[:, l, m, :], xs[:, 2 * m:2 * m + D],
                                   start=(m == 0), stop=(m == 2))
                mm.then_inc(conv_done, 1)

            def step(n, o, tok, prs, att):
                b, p, a = 2 * n + o, 2 * n + o - 1, 2 * n + o - 2
                e = o % 2

                def conv_layer(l):
                    if tok:
                        pe.wait_ge(x_top, 5 * b + l + 1)
                        pe.wait_ge(x_bot, 5 * b + l + 1)
                        conv(l)

                def chunk(c):
                    if not prs:
                        return
                    pe.wait_ge(pair_done, NCH * p + c + 1)
                    at_least(pe, r2_done, NCH * p + c - 1)
                    z = Z[c % 2]
                    for m in range(2):
                        mm = pe.matmul(z[PG * m:PG * m + PG, 0:CW], w2[:, :],
                                       pair[:, c % 4, :, HALF * m:HALF * m + HALF], start=True, stop=True)
                    mm.then_inc(z_done, 1)
                    if c:
                        third(c - 1)

                def third(c):
                    if not prs:
                        return
                    pe.wait_ge(r2_done, NCH * p + c + 1)
                    if c == 0:
                        at_least(pe, sim16_done, p)
                    pe.matmul(W[0:16, 0:CW], w3[:, 7 - c:23 - c], r2[:, c % 2, :],
                              start=(c == 0), stop=(c == NCH - 1)).then_inc(w3_done, 1)

                if tok:
                    pe.wait_ge(enc_in[e], 16 * n + 16 if o < 2 else 16 * n + 32)
                    for s in range(2):
                        mm = pe.matmul(Y[:, s * T:s * T + T], up_w[:, s, :], enc[0:CC, e, :], start=True, stop=True)
                    mm.then_inc(up_done, 1)
                    at_least(pe, h_done, b)
                    for q in range(2):
                        mm = pe.matmul(C[:, q * T:q * T + T], cond_w[:, 128 * q:128 * q + 128], enc[:, e, :],
                                       start=True, stop=True)
                    mm.then_inc(cond_done, 1)
                conv_layer(0)
                if prs:
                    pe.wait_ge(xn_done, p + 1)
                    for k in range(KD):
                        mm = pe.transpose(X[:, S * k:S * k + S], xn[:, 128 * k:128 * k + 128], ident[0:S, 0:S])
                    mm.then_inc(xnT_psum, 1)
                    pe.wait_ge(xnT_done, p + 1)
                    for k in range(KD):
                        mm = pe.matmul(X[:, KD * S:KD * S + S], w1[:, k, :], xnT[:, k, :],
                                       start=(k == 0), stop=(k == KD - 1))
                    mm.then_inc(hT_psum, 1)
                    for k in range(KD):
                        mm = pe.matmul(G[0:S, 1, 0:3 * KQ], xnT[:, k, :], wqkv[:, k, :],
                                       start=(k == 0), stop=(k == KD - 1))
                    mm.then_inc(qkv_psum, 1)
                chunk(0)
                chunk(1)
                conv_layer(1)
                chunk(2)
                chunk(3)
                conv_layer(2)
                if att:
                    pe.wait_ge(pick_done, a + 1)
                    pe.wait_ge(qkv_done, (a + 2) if prs else (a + 1))
                    at_least(pe, h1_done, a)
                    for r in range(TOPK):
                        mm = pe.matmul(G[0:S, r // 4, 128 * (r % 4):128 * (r % 4) + 128], pick[:, r, :],
                                       qkv[:, e, KQ:3 * KQ], start=True, stop=True)
                    mm.then_inc(g_done, 1)
                chunk(4)
                chunk(5)
                conv_layer(3)
                chunk(6)
                if att:
                    pe.wait_ge(ao_done, a + 1)
                    pe.transpose(G[:, 1, 0:S], aon[:, :], ident[0:S, 0:S]).then_inc(aoT_psum, 1)
                chunk(7)
                if tok:
                    pe.wait_ge(x_top, 5 * b + 5)
                    pe.wait_ge(soft_done, b + 1)
                    pe.matmul(C[0:S, 0:D], tok_w[:, :], xs[0:CC, 2:2 + D], start=True, stop=True).then_inc(tok_done, 1)
                if att:
                    pe.wait_ge(aoT_done, a + 1)
                    pe.matmul(G[0:S, 0, 0:D], aoT[:, :], wout[:, :], start=True, stop=True).then_inc(wo_done, 1)
                third(NCH - 1)
            schedule(pe, step)

        @block.scalar
        def _(act):
            act.wait_ge(w_in, 16 * 37)
            act.wait_ge(bn_ready, 3)

            def step(n, o, tok, prs, att):
                b, p, a = 2 * n + o, 2 * n + o - 1, 2 * n + o - 2
                e = o % 2

                def gate(l):
                    if tok:
                        act.wait_ge(conv_done, 4 * b + l + 1)
                        act.activation(th[CC:, :], Y[0:CC, 0:D], ACT.Tanh, bias=gate_b[:, l:l + 1],
                                       scale=0.5).then_inc(th_done, 1)

                def top_copy(l):
                    if tok:
                        act.wait_ge(x_bot, 5 * b + l + 2)
                        act.activation(xs[0:CC, 2:2 + D], xs[CC:, 1:1 + D], ACT.Copy).then_inc(x_top, 1)

                def relu(c):
                    if prs:
                        act.wait_ge(z_done, NCH * p + c + 1)
                        at_least(act, w3_done, NCH * p + c - 1)
                        act.activation(r2[:, c % 2, :], Z[c % 2][:, 0:CW], ACT.Relu, bias=b2[:, :]).then_inc(r2_done, 1)

                if tok:
                    act.wait_ge(up_done, b + 1)
                    for half, sig in ((0, x_top), (1, x_bot)):
                        q = slice(CC * half, CC * half + CC)
                        act.activation(xs[q, 2 - half:2 - half + D].rearrange("p (t s) -> p t s", s=2),
                                       Y[q, :].rearrange("p (s t) -> p t s", s=2), ACT.Relu,
                                       bias=up_shift[q, :], scale=up_scale[q, :]).then_inc(sig, 1)
                    act.wait_ge(cond_done, b + 1)
                    act.activation(cabs[:, :], C[:, :], ACT.Abs).then_inc(abs_done, 1)
                gate(0)
                top_copy(0)
                if prs:
                    act.wait_ge(xnT_psum, p + 1)
                    for k in range(KD):
                        ins = act.activation(xnT[:, k, :], X[:, S * k:S * k + S], ACT.Identity,
                                             bias=beta[:, k:k + 1], scale=gamma[:, k:k + 1])
                    ins.then_inc(xnT_done, 1)
                relu(0)
                relu(1)
                gate(1)
                top_copy(1)
                relu(2)
                relu(3)
                gate(2)
                top_copy(2)
                if att:
                    act.wait_ge(exp_in, a + 1)
                    act.activation(prob[:, :, :], score[:, :, :], ACT.Exp, scale=HD ** -0.5).then_inc(exp_done, 1)
                relu(4)
                relu(5)
                gate(3)
                top_copy(3)
                relu(6)
                if att:
                    act.wait_ge(aoT_psum, a + 1)
                    act.activation(aoT[0:KQ, :], G[0:KQ, 1, 0:S], ACT.Copy).then_inc(aoT_done, 1)
                relu(7)
                if tok:
                    act.wait_ge(tok_done, b + 1)
                    at_least(act, hx_done, b)
                    act.activation(h[:, :], C[0:S, 0:D], ACT.Identity, bias=tok_b[:, :]).then_inc(h_done, 1)
                if prs:
                    act.wait_ge(w3_done, NCH * p + NCH)
                    at_least(act, sim_out, 16 * p)
                    act.activation(sim16[:, :], W[0:16, 0:CW], ACT.Identity, bias=b3[:, :]).then_inc(sim16_done, 1)
            schedule(act, step)

        @block.vector
        def _(dve):
            dve.memset(xs[:, :], 0.0)
            dve.memset(off_diag[:, :], 1.0)
            dve.memset(aon[:, :], 0.0)
            dve.memset(conv_w[CC:, :, 2, :], 0.0)
            dve.memset(w3[:, :], 0.0)
            dve.memset(enc[CC:CC + 1, :, :], 1.0)
            dve.memset(aoT[KQ:KQ + 1, :], 1.0)
            dve.memset(minus_half[:, :], -0.5)
            dve.memset(ident[:, :], 0.0).then_inc(zeros_set, 1)
            dve.wait_ge(w_in, 16 * 37)
            dve.wait_ge(const_chain, 2)
            dve.tensor_scalar(gate_b[:, :], gate_b[:, :], 0.5, None, ALU.mult).then_inc(bn_ready, 1)
            dve.tensor_tensor(up_scale[:, :], bn[:, 1:2], bn[:, 5:6], ALU.mult).then_inc(bn_ready, 1)
            dve.tensor_tensor(up_shift[:, :], bn[:, 0:1], bn[:, 3:4], ALU.subtract).then_inc(const_chain, 1)
            dve.wait_ge(bn_ready, 2)
            dve.wait_ge(const_chain, 3)
            dve.scalar_tensor_tensor(up_shift[:, :], up_shift[:, :], up_scale[:, 0:1], bn[:, 2:3],
                                     ALU.mult, ALU.add).then_inc(bn_ready, 1)

            def step(n, o, tok, prs, att):
                b, p, a = 2 * n + o, 2 * n + o - 1, 2 * n + o - 2
                e = o % 2

                def conv_out(l):
                    if not tok:
                        return
                    q = slice(CC * (l % 2), CC * (l % 2) + CC)
                    dve.wait_ge(conv_done, 4 * b + l + 1)
                    dve.tensor_tensor(lin[CC:, :].rearrange("p (t s) -> p t s", s=2),
                                      Y[CC:, 0:D].rearrange("p (t s) -> p t s", s=2),
                                      cond[q, l // 2, :].unsqueeze(2).to_broadcast([CC, T, 2]),
                                      ALU.add).then_inc(lin_done, 1)
                    dve.wait_ge(lin_done, 4 * b + l + 1)
                    dve.wait_ge(th_done, 4 * b + l + 1)
                    dve.scalar_tensor_tensor(gated[CC:, :], th[CC:, :], 1.0, lin[CC:, :],
                                             ALU.add, ALU.mult).then_inc(gated_done, 1)
                    dve.wait_ge(gated_done, 4 * b + l + 1)
                    dve.scalar_tensor_tensor(xs[CC:, 1:1 + D], gated[CC:, :], 0.5, xs[CC:, 1:1 + D],
                                             ALU.mult, ALU.add).then_inc(x_bot, 1)

                def pairs(c, lo=0, hi=CH):
                    if not prs:
                        return
                    if lo == 0:
                        at_least(dve, z_done, NCH * p + c - 3)
                    for i in range(lo, hi):
                        g = CH * c + i
                        ins = dve.tensor_scalar(pair[:, c % 4, i, :], hm[:, :], hp[:, g:g + 1], 0.0,
                                                ALU.add, ALU.max)
                    if hi == CH:
                        ins.then_inc(pair_done, 1)

                def stats_of(k, src):
                    dve.bn_stats(stats[:, k, :], src).then_inc(ln_chain, 1)

                def variance(k):
                    dve.bn_aggr(mv[:, k, :], stats[:, k, :]).then_inc(ln_chain, 1)
                    dve.wait_ge(ln_chain, 4 * b + 2 * k + 2)
                    dve.tensor_scalar(veps[:, k:k + 1], mv[:, k, 1:2], LN_EPS, None, ALU.add).then_inc(veps_done, 1)

                if tok:
                    dve.wait_ge(abs_done, b + 1)
                    dve.tensor_scalar(cabs[:, :], cabs[:, :], 1.0, None, ALU.add).then_inc(soft_done_chain, 1)
                    dve.wait_ge(soft_done_chain, 3 * b + 1)
                    dve.reciprocal(cabs[:, :], cabs[:, :]).then_inc(soft_done_chain, 1)
                    dve.wait_ge(soft_done_chain, 3 * b + 2)
                    dve.tensor_tensor(cond[:, :, :].rearrange("p q t -> p (q t)"), C[:, :], cabs[:, :],
                                      ALU.mult).then_inc(soft_done, 1)
                    dve.wait_ge(soft_done, b + 1)
                    for q in range(2):
                        ins = dve.tensor_scalar(cond[:, q, :], cond[:, q, :], lin_b[:, q:q + 1], None, ALU.add)
                    ins.then_inc(soft_done_chain, 1)
                    dve.wait_ge(soft_done_chain, 3 * b + 3)
                conv_out(0)
                if prs:
                    dve.wait_ge(hT_psum, p + 1)
                    hT = X[:, KD * S:KD * S + S]
                    dve.tensor_scalar(hp[:, :], hT, b1[:, 0:1], None, ALU.add).then_inc(hpm_done, 1)
                    dve.tensor_scalar(hm[:, :], hT, -1.0, None, ALU.mult).then_inc(hpm_done, 1)
                    dve.wait_ge(hpm_done, 2 * p + 2)
                pairs(0)
                pairs(1)
                if prs:
                    dve.wait_ge(qkv_psum, p + 1)
                    dve.tensor_tensor(qkv[:, (e + 1) % 2, :], G[0:S, 1, 0:3 * KQ], bqkv[:, :],
                                      ALU.add).then_inc(qkv_done, 1)
                pairs(2)
                pairs(3, 0, CH - 6)
                if att:
                    dve.wait_ge(sim_done, a + 1)
                pairs(3, CH - 6, CH - 5)
                if att:
                    dve.max(top[:, :], sim[:, :]).then_inc(top_done, 1)
                pairs(3, CH - 5, CH - 1)
                if att:
                    dve.wait_ge(top_done, a + 1)
                pairs(3, CH - 1, CH)
                if att:
                    dve.max_index(idx[:, :], top[:, :], sim[:, :]).then_inc(idx_done, 1)
                conv_out(1)
                pairs(4)
                pairs(5)
                conv_out(2)
                if att:
                    dve.wait_ge(idx_back, 16 * a + 16)
                    dve.tensor_scalar(pick[:, :, :], idx_all[:, :, :].rearrange("j i r -> j r i"), key_no[:, 0:1],
                                      None, ALU.is_equal).then_inc(pick_done, 1)
                pairs(6)
                if att:
                    dve.wait_ge(g_done, a + 1)
                    gk = G[0:S, :, :].rearrange("i m (r c) -> i (m r) c", c=2 * KQ)
                    dve.tensor_tensor(prod[:, :, :], gk[:, :, 0:KQ],
                                      qkv[:, e, 0:KQ].unsqueeze(1).to_broadcast([S, TOPK, KQ]),
                                      ALU.mult).then_inc(at_chain, 1)
                    dve.wait_ge(at_chain, 7 * a + 1)
                    pr = prod[:, :, :].rearrange("i r (h d) -> i r h d", d=HD)
                    dve.tensor_tensor(score[:, :, :], pr[:, :, :, 0], pr[:, :, :, 1], ALU.add).then_inc(at_chain, 1)
                    dve.wait_ge(at_chain, 7 * a + 2)
                    dve.tensor_reduce(smax[:, :], score[:, :, :].rearrange("i r h -> i h r"), AX.X,
                                      ALU.max).then_inc(at_chain, 1)
                    dve.wait_ge(at_chain, 7 * a + 3)
                    dve.tensor_tensor(score[:, :, :], score[:, :, :],
                                      smax[:, :].unsqueeze(1).to_broadcast([S, TOPK, NH]),
                                      ALU.subtract).then_inc(exp_in, 1)
                pairs(7)
                if att:
                    dve.wait_ge(exp_done, a + 1)
                    dve.tensor_reduce(psum_[:, :], prob[:, :, :].rearrange("i r h -> i h r"), AX.X,
                                      ALU.add).then_inc(at_chain, 1)
                    for d in range(HD):
                        ins = dve.tensor_tensor(pv[:, :, :].rearrange("i r (h d) -> i r h d", d=HD)[:, :, :, d],
                                                gk[:, :, KQ:].rearrange("i r (h d) -> i r h d", d=HD)[:, :, :, d],
                                                prob[:, :, :], ALU.mult)
                    ins.then_inc(at_chain, 1)
                    dve.wait_ge(at_chain, 7 * a + 4)
                    dve.reciprocal(pinv[:, :], psum_[:, :]).then_inc(at_chain, 1)
                    dve.wait_ge(at_chain, 7 * a + 5)
                    dve.tensor_reduce(ao[:, :], pv[:, :, :].rearrange("i r c -> i c r"), AX.X,
                                      ALU.add).then_inc(at_chain, 1)
                    dve.wait_ge(at_chain, 7 * a + 7)
                    dve.tensor_tensor(aon[:, 0:KQ].rearrange("i (h d) -> i h d", d=HD),
                                      ao[:, :].rearrange("i (h d) -> i h d", d=HD),
                                      pinv[:, :].unsqueeze(2).to_broadcast([S, NH, HD]), ALU.mult).then_inc(ao_done, 1)
                conv_out(3)
                if tok:
                    dve.wait_ge(h_done, b + 1)
                    stats_of(0, h[:, :])
                if att:
                    dve.wait_ge(wo_done, a + 1)
                if tok:
                    dve.wait_ge(ln_chain, 4 * b + 1)
                if att:
                    dve.tensor_tensor(h1[:, :], G[0:S, 0, 0:D], hx[:, e, :], ALU.add).then_inc(h1_done, 1)
                if tok:
                    variance(0)
                    dve.wait_ge(rstd_done, 2 * b + 1)
                    dve.tensor_scalar(xa[:, :], h[:, :], mv[:, 0, 0:1], rstd[:, 0:1], ALU.subtract,
                                      ALU.mult).then_inc(xa_done, 1)
                    dve.wait_ge(xa_done, b + 1)
                    stats_of(1, xa[:, :])
                    dve.wait_ge(ln_chain, 4 * b + 3)
                    dve.tensor_tensor(hx[:, e, :], h[:, :], xa[:, :], ALU.add).then_inc(hx_done, 1)
                    variance(1)
                    dve.wait_ge(rstd_done, 2 * b + 2)
                    at_least(dve, xnT_psum, b)
                    dve.tensor_scalar(xn[:, :], xa[:, :], mv[:, 1, 0:1], rstd[:, 1:2], ALU.subtract,
                                      ALU.mult).then_inc(xn_done, 1)
            soft_done_chain = sem("soft_done_chain")
            xa_done = sem("xa_done")
            schedule(dve, step)


def experts(nc, t):
    N, D = t["h1f"].shape
    KD = D // 128
    E = t["gateT"].shape[1] - 1
    FS = t["sdT"].shape[0]
    I = t["edT"].shape[1]
    NT = 512
    TT = NT // 128
    ST = N // NT
    IH = I // 2
    SF = FS // 128
    with ExitStack() as ctx:
        def sb(name, shape, dt=F32):
            return ctx.enter_context(nc.sbuf_tensor("q_" + name, shape, dt))

        def sem(name):
            return ctx.enter_context(nc.semaphore("q_" + name))
        sg_w = sb("sg_w", [128, KD, FS])
        su_w = sb("su_w", [128, KD, FS])
        sd_w = sb("sd_w", [128, SF, D])
        eg_w = sb("eg_w", [128, KD, E, 2 * I])
        ed_w = sb("ed_w", [IH, E, 2, D])
        rt_w = sb("rt_w", [128, KD, E + 1])
        ident = sb("ident", [128, 128])
        sel = sb("sel", [E + 1, E + 1, 128])
        minus_half = sb("minus_half", [128, TT])
        e_no = sb("e_no", [128, E])
        hin = sb("hin", [128, TT, D])
        xn = sb("xn", [128, TT, D])
        xT = sb("xT", [128, KD, NT])
        stats = sb("stats", [128, TT, 6])
        mv = sb("mv", [128, TT, 2])
        veps = sb("veps", [128, TT])
        rstd = sb("rstd", [128, TT])
        lg = sb("lg", [128, TT, E + 1])
        lmax = sb("lmax", [128, TT])
        pr = sb("pr", [128, TT, E])
        psm = sb("psm", [128, TT])
        top = sb("top", [128, TT, 8])
        idx = sb("idx", [128, TT, 8], U32)
        one = sb("one", [128, 2, TT, E])
        cw = sb("cw", [128, TT, E + 1])
        cwT = sb("cwT", [E + 1, NT])
        cwb = sb("cwb", [128, E + 1, NT])
        nudge = sb("nudge", [128, 1])
        th = sb("th", [128, 2, NT])
        act_ = sb("act_", [128, 2, NT])
        bank = [ctx.enter_context(nc.psum_tensor(f"q_bank{i}", [128, 512], F32)) for i in range(8)]
        GU, OUT = bank[0:4], bank[4:8]

        w_in, consts, zeros = sem("w_in"), sem("consts"), sem("zeros")
        h_in, out_done, out_out = sem("h_in"), sem("out_done"), sem("out_out")
        ln, veps_done, rstd_done, xn_done, xT_psum, xT_done = [sem(x) for x in ("ln", "veps", "rstd", "xn", "xTp", "xTd")]
        lg_psum, rt, exp_in, exp_done, sg_done, cw_done = [sem(x) for x in ("lgp", "rt", "expi", "expd", "sgd", "cwd")]
        cwT_psum, cwT_done, cwb_psum, cwb_done = [sem(x) for x in ("cwTp", "cwTd", "cwbp", "cwbd")]
        gu_done, th_done, a1, act_done, down_done, all_done = [sem(x) for x in ("gu", "th", "a1", "act", "down", "all")]
        block = ctx.enter_context(nc.Block())
        NW = 6
        F = SF + 2 * E
        tiles = [("s", f, 128) for f in range(SF)] + [("e", f, IH) for f in range(2 * E)]

        def schedule(eng, step):
            step(0)
            with eng.Fori(1, ST) as n:
                step(n)

        @block.sync
        def _(sp):
            sp.dma_start(rt_w[:, :, :], t["gateT"].rearrange("(k p) f -> p k f", p=128)).then_inc(w_in, 16)
            sp.dma_start(sg_w[:, :, :], t["sgT"].rearrange("(k p) f -> p k f", p=128)).then_inc(w_in, 16)
            sp.dma_start(su_w[:, :, :], t["suT"].rearrange("(k p) f -> p k f", p=128)).then_inc(w_in, 16)
            sp.dma_start(sd_w[:, :, :], t["sdT"].rearrange("(k p) f -> p k f", p=128)).then_inc(w_in, 16)
            sp.dma_start(eg_w[:, :, :, :].rearrange("p k e f -> p k (e f)"), t["egT"].rearrange("(k p) e f -> p k (e f)", p=128)).then_inc(w_in, 16)
            sp.dma_start(ed_w[:, :, :, :], t["edT"].rearrange("e (h p) d -> p e h d", p=IH)).then_inc(w_in, 16)

            def step(n):
                at_least(sp, out_out, 16 * n)
                src = t["h1f"][n * NT:n * NT + NT] if isinstance(n, int) else t["h1f"][bass.ds(n * NT, NT)]
                dst = t["out"][n * NT:n * NT + NT] if isinstance(n, int) else t["out"][bass.ds(n * NT, NT)]
                sp.dma_start(hin[:, :, :], src.rearrange("(a p) d -> p a d", p=128)).then_inc(h_in, 16)
                sp.wait_ge(out_done, TT * n + TT)
                sp.dma_start(dst.rearrange("(a p) d -> p a d", p=128), hin[:, :, :]).then_inc(out_out, 16)
            schedule(sp, step)
            sp.wait_ge(out_out, 16 * ST)

        @block.gpsimd
        def _(pool):
            pool.iota(e_no[:, :], [[1, E]], base=0, channel_multiplier=0,
                      allow_small_or_imprecise_dtypes=True).then_inc(consts, 1)
            pool.wait_ge(zeros, 1)
            pool.affine_select(out=ident[:, :], in_=ident[:, :], compare_op=ALU.not_equal, fill=1.0,
                               base=0, pattern=[[-1, 128]], channel_multiplier=1).then_inc(consts, 1)
            pool.affine_select(out=sel[:, :, :], in_=sel[:, :, :], compare_op=ALU.not_equal, fill=1.0,
                               base=0, pattern=[[-1, E + 1], [0, 128]], channel_multiplier=1).then_inc(consts, 1)

            def step(n):
                pool.wait_ge(veps_done, n + 1)
                pool.tensor_tensor(rstd[:, :], veps[:, :], minus_half[:, :], ALU.pow).then_inc(rstd_done, 1)
            schedule(pool, step)

        @block.tensor
        def _(pe):
            pe.wait_ge(consts, 3)
            pe.wait_ge(w_in, 16 * NW)

            def down(n, j):
                kind, f, m = tiles[j]
                pe.wait_ge(act_done, F * n + j + 1)
                if j == 0:
                    at_least(pe, out_done, TT * n)
                w = sd_w[:, f, :] if kind == "s" else ed_w[:, f // 2, f % 2, :]
                for a in range(TT):
                    mm = pe.matmul(OUT[a][:, 0:D], act_[0:m, j % 2, 128 * a:128 * a + 128], w,
                                   start=(j == 0), stop=(j == F - 1))
                mm.then_inc(down_done, 1)

            def step(n):
                pe.wait_ge(xn_done, n + 1)
                for k in range(KD):
                    for a in range(TT):
                        mm = pe.transpose(GU[k][:, 128 * a:128 * a + 128], xn[:, a, 128 * k:128 * k + 128], ident[:, :])
                    mm.then_inc(xT_psum, 1)
                pe.wait_ge(xT_done, KD * n + KD)
                for a in range(TT):
                    for k in range(KD):
                        mm = pe.matmul(GU[0][:, 16 * a:16 * a + E + 1], xT[:, k, 128 * a:128 * a + 128], rt_w[:, k, :],
                                       start=(k == 0), stop=(k == KD - 1))
                mm.then_inc(lg_psum, 1)
                pe.wait_ge(cw_done, 2 * n + 2)
                for a in range(TT):
                    mm = pe.transpose(GU[1][0:E + 1, 128 * a:128 * a + 128], cw[:, a, :], ident[:, :])
                mm.then_inc(cwT_psum, 1)
                pe.wait_ge(cwT_done, n + 1)
                for q in range(E + 1):
                    at_least(pe, cwb_done, (E + 1) * n + q - 1)
                    pe.matmul(GU[2 + q % 2][:, :], sel[:, q, :], cwT[:, :], start=True, stop=True).then_inc(cwb_psum, 1)
                pe.wait_ge(cwb_done, (E + 1) * n + E + 1)
                for j, (kind, f, m) in enumerate(tiles):
                    if j >= 2:
                        pe.wait_ge(act_done, F * n + j - 1)
                    for h in range(2):
                        for k in range(KD):
                            if kind == "s":
                                w = (su_w if h else sg_w)[:, k, 128 * f:128 * f + 128]
                            else:
                                c = I * h + IH * (f % 2)
                                w = eg_w[:, k, f // 2, c:c + IH]
                            mm = pe.matmul(GU[2 * (j % 2) + h][0:m, :], w, xT[:, k, :], start=(k == 0), stop=(k == KD - 1))
                        mm.then_inc(gu_done, 1)
                    if j:
                        down(n, j - 1)
                down(n, F - 1)
            schedule(pe, step)

        @block.scalar
        def _(act):
            def step(n):
                for k in range(KD):
                    act.wait_ge(xT_psum, KD * n + k + 1)
                    act.activation(xT[:, k, :], GU[k][:, :], ACT.Copy).then_inc(xT_done, 1)
                act.wait_ge(lg_psum, n + 1)
                act.activation(lg[:, :, :], GU[0][:, 0:16 * TT].rearrange("p (a e) -> p a e", e=16)[:, :, 0:E + 1], ACT.Copy).then_inc(rt, 1)
                act.wait_ge(exp_in, n + 1)
                act.activation(pr[:, :, :], pr[:, :, :], ACT.Exp).then_inc(exp_done, 1)
                act.activation(cw[:, :, E:E + 1], lg[:, :, E:E + 1], ACT.Tanh, scale=0.5).then_inc(sg_done, 1)
                act.wait_ge(cwT_psum, n + 1)
                act.activation(cwT[:, :], GU[1][0:E + 1, :], ACT.Copy, scale=0.5).then_inc(cwT_done, 1)
                for q in range(E + 1):
                    act.wait_ge(cwb_psum, (E + 1) * n + q + 1)
                    act.activation(cwb[:, q, :], GU[2 + q % 2][:, :], ACT.Copy).then_inc(cwb_done, 1)
                for j, (kind, f, m) in enumerate(tiles):
                    act.wait_ge(gu_done, 2 * (F * n + j) + 1)
                    at_least(act, act_done, F * n + j - 1)
                    act.activation(th[0:m, j % 2, :], GU[2 * (j % 2)][0:m, :], ACT.Tanh, scale=0.5).then_inc(th_done, 1)
            schedule(act, step)

        @block.vector
        def _(dve):
            dve.memset(ident[:, :], 0.0)
            dve.memset(minus_half[:, :], -0.5)
            dve.memset(sel[:, :, :], 0.0).then_inc(zeros, 1)

            def chain(s, n, k, per):
                dve.wait_ge(s, per * n + k)

            def step(n):
                dve.wait_ge(h_in, 16 * n + 16)
                for a in range(TT):
                    dve.bn_stats(stats[:, a, :], hin[:, a, :]).then_inc(ln, 1)
                dve.wait_ge(ln, 2 * TT * n + TT)
                dve.memset(nudge[:, :], 0.0)
                for a in range(TT):
                    dve.bn_aggr(mv[:, a, :], stats[:, a, :]).then_inc(ln, 1)
                dve.wait_ge(ln, 2 * TT * n + 2 * TT)
                dve.tensor_scalar(veps[:, :], mv[:, :, 1], LN_EPS, None, ALU.add).then_inc(veps_done, 1)
                dve.wait_ge(rstd_done, n + 1)
                for a in range(TT):
                    ins = dve.tensor_scalar(xn[:, a, :], hin[:, a, :], mv[:, a, 0:1], rstd[:, a:a + 1],
                                            ALU.subtract, ALU.mult)
                ins.then_inc(xn_done, 1)
                dve.wait_ge(rt, n + 1)
                dve.tensor_reduce(lmax[:, :], lg[:, :, 0:E], AX.X, ALU.max).then_inc(a1, 1)
                K = 8 + F * 2
                dve.wait_ge(a1, K * n + 1)
                dve.tensor_tensor(pr[:, :, :], lg[:, :, 0:E], lmax[:, :].unsqueeze(2).to_broadcast([128, TT, E]),
                                  ALU.subtract).then_inc(exp_in, 1)
                dve.wait_ge(exp_done, n + 1)
                dve.tensor_reduce(psm[:, :], pr[:, :, :], AX.X, ALU.add).then_inc(a1, 1)
                dve.wait_ge(a1, K * n + 2)
                dve.reciprocal(psm[:, :], psm[:, :]).then_inc(a1, 1)
                dve.wait_ge(a1, K * n + 3)
                dve.tensor_tensor(pr[:, :, :], pr[:, :, :], psm[:, :].unsqueeze(2).to_broadcast([128, TT, E]),
                                  ALU.mult).then_inc(a1, 1)
                dve.wait_ge(a1, K * n + 4)
                dve.memset(nudge[:, :], 0.0)
                for a in range(TT):
                    ins = dve.max(top[:, a, :], pr[:, a, :])
                ins.then_inc(a1, 1)
                dve.wait_ge(a1, K * n + 5)
                dve.memset(nudge[:, :], 0.0)
                for a in range(TT):
                    ins = dve.max_index(idx[:, a, :], top[:, a, :], pr[:, a, :])
                ins.then_inc(a1, 1)
                dve.tensor_tensor(psm[:, :], top[:, :, 0], top[:, :, 1], ALU.add).then_inc(a1, 1)
                dve.wait_ge(a1, K * n + 7)
                dve.reciprocal(psm[:, :], psm[:, :])
                for k in range(2):
                    ins = dve.tensor_tensor(one[:, k, :, :], e_no[:, :].unsqueeze(1).to_broadcast([128, TT, E]),
                                            idx[:, :, k:k + 1].to_broadcast([128, TT, E]), ALU.is_equal)
                ins.then_inc(a1, 1)
                dve.wait_ge(a1, K * n + 8)
                dve.tensor_tensor(one[:, 0, :, :], one[:, 0, :, :], one[:, 1, :, :], ALU.add).then_inc(r2, 1)
                dve.tensor_tensor(pr[:, :, :], pr[:, :, :], psm[:, :].unsqueeze(2).to_broadcast([128, TT, E]),
                                  ALU.mult).then_inc(r2, 1)
                dve.wait_ge(r2, 2 * n + 2)
                dve.tensor_tensor(cw[:, :, 0:E], pr[:, :, :], one[:, 0, :, :], ALU.mult).then_inc(cw_done, 1)
                dve.wait_ge(sg_done, n + 1)
                dve.tensor_scalar(cw[:, :, E:E + 1], cw[:, :, E:E + 1], 1.0, 0.5, ALU.add, ALU.mult).then_inc(cw_done, 1)
                for j, (kind, f, m) in enumerate(tiles):
                    q = E if kind == "s" else f // 2
                    dve.wait_ge(th_done, F * n + j + 1)
                    at_least(dve, down_done, F * n + j - 1)
                    x = act_[0:m, j % 2, :]
                    dve.scalar_tensor_tensor(x, th[0:m, j % 2, :], 1.0, GU[2 * (j % 2)][0:m, :], ALU.add,
                                             ALU.mult).then_inc(a1, 1)
                    dve.wait_ge(a1, K * n + 9 + 2 * j)
                    dve.wait_ge(gu_done, 2 * (F * n + j) + 2)
                    dve.tensor_tensor(x, x, GU[2 * (j % 2) + 1][0:m, :], ALU.mult).then_inc(a1, 1)
                    dve.wait_ge(a1, K * n + 10 + 2 * j)
                    dve.tensor_tensor(x, x, cwb[0:m, q, :], ALU.mult).then_inc(act_done, 1)
                dve.wait_ge(down_done, F * n + F)
                for a in range(TT):
                    dve.tensor_tensor(hin[:, a, :], OUT[a][:, :], hin[:, a, :], ALU.add).then_inc(out_done, 1)
            r2 = sem("r2")
            schedule(dve, step)


def program(nc, t):
    B, S, D = t["out"].shape
    scratch = nc.dram_tensor("h1_d", (B, S, D), F32, kind="Internal").ap()
    t["h1"] = scratch
    t["h1f"] = scratch.rearrange("b s d -> (b s) d")
    tokens_and_attention(nc, t)
    t["out"] = t["out"].rearrange("b s d -> (b s) d")
    experts(nc, t)


def kernel(**inputs):
    import numpy as np
    import concourse.bacc as bacc
    from concourse.bass_utils import run_bass_kernel_spmd as run

    i = {k: np.asarray(v) for k, v in inputs.items()}
    tok = {k[7:]: v for k, v in i.items() if k.startswith("L0_tok_")}
    att = {k[8:]: v for k, v in i.items() if k.startswith("L0_attn_")}
    ffn = {k[7:]: v for k, v in i.items() if k.startswith("L0_ffn_")}
    x = i["x"].transpose(0, 2, 1)
    CI = tok["up_b"].shape[0]
    D, L = att["gamma"].shape[0], tok["conv_bs"].shape[0]

    def col(a):
        return a.reshape(-1, 1)

    laid = {
        "xT": np.concatenate([x, x[:1]]),
        "up_wT": tok["up_w"].transpose(0, 2, 1),
        "convT": tok["conv_ws"].transpose(3, 2, 0, 1),
        "gate_b": tok["conv_bs"][:, :CI].T,
        "lin_b": tok["conv_bs"][:, CI:].reshape(L // 2, 2, CI).transpose(1, 2, 0).reshape(2 * CI, L // 2),
        "condT": tok["cond_ws"].transpose(2, 0, 1).reshape(-1, L * CI),
        "cond_b": tok["cond_bs"].reshape(1, L * CI),
        "out_wT": tok["out_w"].T,
        "out_b": col(tok["out_b"]),
        "up_b": col(tok["up_b"]),
        "bn_gamma": col(tok["bn_gamma"]),
        "bn_beta": col(tok["bn_beta"]),
        "bn_mean": col(tok["bn_mean"]),
        "bn_var": col(tok["bn_var"]),
        "gamma": att["gamma"].reshape(D // 128, 128).T,
        "beta": att["beta"].reshape(D // 128, 128).T,
        "W1T": att["W1"].T,
        "b1": col(att["b1"]),
        "W2T": att["W2"].T,
        "b2": col(att["b2"]),
        "W3T": att["W3"].T,
        "b3": att["b3"],
        "WqkvT": att["Wqkv"].T,
        "bqkv": att["bqkv"],
        "WoutT": att["Wout"].T,
        "bout": att["bout"].reshape(1, D),
        "gateT": np.concatenate([ffn["gate_w"], ffn["shared_expert_gate_w"]]).T,
        "sgT": ffn["shared_gate_w"].T,
        "suT": ffn["shared_up_w"].T,
        "sdT": ffn["shared_down_w"].T,
        "egT": ffn["gate_up_proj"].transpose(2, 0, 1),
        "edT": ffn["down_proj"].transpose(0, 2, 1),
    }
    nc = bacc.Bacc("TRN2", target_bir_lowering=False, num_devices=1)
    arrays, t = {}, {}
    for name, a in laid.items():
        a = np.ascontiguousarray(a)
        arrays[f"in_{name}"] = a
        t[name] = nc.dram_tensor(f"in_{name}", a.shape, mybir.dt.from_np(a.dtype), kind="ExternalInput").ap()
    shape = (x.shape[0], tok["out_b"].shape[0], 2 * x.shape[2])
    t["out"] = nc.dram_tensor("out_0", shape, F32, kind="ExternalOutput").ap()
    program(nc, t)
    r = run(nc, [arrays], core_ids=[0])
    return r.results[0]["out_0"]
```

```python
import concourse.bass as bass
from concourse import mybir
from contextlib import ExitStack

F32 = mybir.dt.float32
U32 = mybir.dt.uint32
ALU = mybir.AluOpType
ACT = mybir.ActivationFunctionType
AX = mybir.AxisListType

BN_EPS = 1e-5
LN_EPS = 1e-5
TOPK = 8


def at_least(eng, sem, value):
    if isinstance(value, int) and value <= 0:
        return
    eng.wait_ge(sem, value)


def tokens_and_attention(nc, t):
    B, CC, T = t["xT"].shape[0] - 2, *t["xT"].shape[1:]
    L, S = 4, t["out_wT"].shape[1]
    D = 2 * T
    KD = D // 128
    HF = t["W1T"].shape[1]
    PG = t["W2T"].shape[1]
    KQ = t["WoutT"].shape[0]
    HD = 2
    NH = KQ // HD
    PAD = D + 4
    GEN = 20
    CH = 10
    NCH = S // CH
    HALF = S // 2
    CW = CH * HALF

    with ExitStack() as ctx:
        def sb(name, shape, dt=F32):
            return ctx.enter_context(nc.sbuf_tensor(name, shape, dt))

        def ps(name, shape):
            return ctx.enter_context(nc.psum_tensor(name, shape, F32))

        def sem(name):
            return ctx.enter_context(nc.semaphore(name))

        up_w = sb("up_w", [CC, 2, 2 * CC])
        bn = sb("bn", [128, 6])
        up_scale = sb("up_scale", [128, 1])
        up_shift = sb("up_shift", [128, 1])
        conv_w = sb("conv_w", [128, L, 3, 128])
        gate_b = sb("gate_b", [64, L])
        lin_b = sb("lin_b", [128, 2])
        cond_w = sb("cond_w", [CC + 1, L * CC])
        tok_w = sb("tok_w", [CC, S])
        tok_b = sb("tok_b", [S, 1])
        gamma = sb("gamma", [128, KD])
        beta = sb("beta", [128, KD])
        w1 = sb("w1", [128, KD, HF])
        b1 = sb("b1", [128, 1])
        w2 = sb("w2", [128, PG])
        b2 = sb("b2", [128, 1])
        w3 = sb("w3", [128, 23])
        b3 = sb("b3", [16, 1])
        wqkv = sb("wqkv", [128, KD, 3 * KQ])
        bqkv = sb("bqkv", [S, 3 * KQ])
        wout = sb("wout", [KQ + 1, D])
        ident = sb("ident", [128, 128])
        key_no = sb("key_no", [S, 1])
        off_diag = sb("off_diag", [S, S])
        minus_half = sb("minus_half", [128, 1])

        enc = sb("enc", [CC + 1, 2, T])
        xs = sb("xs", [128, PAD])
        cabs = sb("cabs", [128, 2 * T])
        soft = sb("soft", [128, 2, T])
        xc = sb("xc", [128, 2, L, D])
        th = sb("th", [128, D])
        gated = sb("gated", [128, D])
        h = sb("h", [S, D])
        xa = sb("xa", [S, D])
        hx = sb("hx", [S, 2, D])
        xn = sb("xn", [S, D])
        stats = sb("stats", [S, 2, 6])
        mv = sb("mv", [S, 2, 2])
        turn = sb("turn", [1, 1])
        veps = sb("veps", [S, 2])
        rstd = sb("rstd", [S, 2])
        xnT = sb("xnT", [128, KD, S])
        hT = sb("hT", [128, S])
        pair = sb("pair", [128, 4, GEN, S])
        r2 = sb("r2", [128, 4, CW])
        sim16 = sb("sim16", [16, CW])
        qkv = sb("qkv", [S, 2, 3 * KQ])
        sim_in = sb("sim_in", [S, S])
        sim = sb("sim", [S, S])
        top = sb("top", [S, TOPK])
        idx = sb("idx", [S, TOPK], U32)
        idx_all = sb("idx_all", [S, S, TOPK], U32)
        pick = sb("pick", [S, TOPK, S])
        prod = sb("prod", [S, TOPK, KQ])
        score = sb("score", [S, TOPK, NH])
        smax = sb("smax", [S, NH])
        prob = sb("prob", [S, TOPK, NH])
        psum_ = sb("psum_", [S, NH])
        pinv = sb("pinv", [S, NH])
        pv = sb("pv", [S, TOPK, KQ])
        ao = sb("ao", [S, KQ])
        aon = sb("aon", [S, 128])
        aoT = sb("aoT", [KQ + 1, S])
        h1 = sb("h1", [S, D])

        Y = ps("Y", [128, 512])
        C = ps("C", [128, 512])
        Z = [ps("Z0", [128, 512]), ps("Z1", [128, 512])]
        W = ps("W", [128, 512])
        G = ps("G", [128, 2, 512])
        X = ps("X", [128, 512])

        sim_d = nc.dram_tensor("sim_d", (16, CW), F32, kind="Internal").ap()
        idx_d = nc.dram_tensor("idx_d", (S, TOPK), U32, kind="Internal").ap()

        w_in = sem("weights_in")
        consts = sem("consts")
        zeros_set = sem("zeros_set")
        const_chain = sem("const_chain")
        bn_ready = sem("bn_ready")
        enc_in = [sem("enc_in0"), sem("enc_in1")]
        up_done, cond_done, conv_done, tok_done = sem("up_done"), sem("cond_done"), sem("conv_done"), sem("tok_done")
        x_top, x_bot, xc_top, crep_done = sem("x_top"), sem("x_bot"), sem("xc_top"), sem("crep_done")
        abs_done, abs1_done, recip_done, soft_done = sem("abs_done"), sem("abs1_done"), sem("recip_done"), sem("soft_done")
        th_done, gated_done = sem("th_done"), sem("gated_done")
        h_done, ln_chain, veps_done, rstd_done = sem("h_done"), sem("ln_chain"), sem("veps_done"), sem("rstd_done")
        xn_done, hx_done = sem("xn_done"), sem("hx_done")
        xnT_psum, xnT_done, hT_psum, hT_done = sem("xnT_psum"), sem("xnT_done"), sem("hT_psum"), sem("hT_done")
        qkv_psum, qkv_done = sem("qkv_psum"), sem("qkv_done")
        diff_done, pair_done, z_done, r2_done, w3_done = sem("diff_done"), sem("pair_done"), sem("z_done"), sem("r2_done"), sem("w3_done")
        sim16_done, sim_out, sim_back, sim_done = sem("sim16_done"), sem("sim_out"), sem("sim_back"), sem("sim_done")
        top_done, idx_done, idx_out, idx_back = sem("top_done"), sem("idx_done"), sem("idx_out"), sem("idx_back")
        pick_done, g_done = sem("pick_done"), sem("g_done")
        at_chain, exp_in, exp_done, ao_done = sem("at_chain"), sem("exp_in"), sem("exp_done"), sem("ao_done")
        aoT_psum, aoT_done, wo_done = sem("aoT_psum"), sem("aoT_done"), sem("wo_done")
        h1_done = sem("h1_done")
        h1_out = sem("h1_out")

        block = ctx.enter_context(nc.Block())

        def schedule(eng, step, start):
            start(0, 0)
            step(0, 0, True, False, False)
            step(0, 1, True, True, False)
            with eng.Fori(1, B // 2) as n:
                step(n, 0, True, True, True)
                step(n, 1, True, True, True)
            step(B // 2, 0, False, True, True)
            step(B // 2, 1, False, False, True)

        @block.sync
        def _(sp):
            loads = [
                (up_w[:, :, 0:CC], t["up_wT"]), (up_w[:, :, CC:], t["up_wT"]),
                (conv_w[0:CC, :, 0, :], t["convT"][0]), (conv_w[CC:, :, 0, :], t["convT"][1]),
                (conv_w[0:CC, :, 1, :], t["convT"][2]), (conv_w[CC:, :, 1, :], t["convT"][3]),
                (conv_w[0:CC, :, 2, :], t["convT"][4]),
                (lin_b[:, :], t["lin_b"]), (cond_w[0:CC, :], t["condT"]), (cond_w[CC:CC + 1, :], t["cond_b"]),
                (tok_w[:, :], t["out_wT"]), (tok_b[:, :], t["out_b"]), (gate_b[:, :], t["gate_b"]),
                (gamma[:, :], t["gamma"]),
                (beta[:, :], t["beta"]),
                (w1[:, :, :], t["W1T"].rearrange("(k p) f -> p k f", p=128)),
                (b1[:, :], t["b1"]), (w2[:, :], t["W2T"]),
                (b2[0:PG, :], t["b2"]), (b2[PG:, :], t["b2"]),
                (w3[0:PG, 7:8], t["W3T"]), (w3[PG:, 15:16], t["W3T"]),
                (b3[:, :], t["b3"].partition_broadcast(16)),
                (wqkv[:, :, :], t["WqkvT"].rearrange("(k p) f -> p k f", p=128)),
                (bqkv[:, :], t["bqkv"].partition_broadcast(S)),
                (wout[0:KQ, :], t["WoutT"]), (wout[KQ:KQ + 1, :], t["bout"]),
            ]
            for i, name in enumerate(["up_b", "bn_gamma", "bn_beta", "bn_mean", "bn_var"]):
                loads += [(bn[0:CC, i:i + 1], t[name]), (bn[CC:, i:i + 1], t[name])]
            sp.wait_ge(zeros_set, 1)
            for k in range(2):
                sp.dma_start(enc[0:CC, k, :], t["xT"][k]).then_inc(enc_in[k], 16)
            for dst, src in loads:
                sp.dma_start(dst, src).then_inc(w_in, 16)

            def step(n, o, tok, prs, att):
                b = 2 * n + o
                if tok:
                    sp.wait_ge(up_done, b + 1)
                    sp.wait_ge(cond_done, b + 1)
                    src = t["xT"][b + 2] if isinstance(n, int) else t["xT"][bass.ds(b + 2, 1)].squeeze(0)
                    sp.dma_start(enc[0:CC, o % 2, :], src).then_inc(enc_in[o % 2], 16)
                if att:
                    a = b - 2
                    sp.wait_ge(idx_done, a + 1)
                    sp.dma_start(idx_d, idx[:, :]).then_inc(idx_out, 16)
                    sp.wait_ge(idx_out, 16 * a + 16)
                    sp.dma_start(idx_all[:, :, :], idx_d.partition_broadcast(S)).then_inc(idx_back, 16)
                if att:
                    a = b - 2
                    sp.wait_ge(h1_done, a + 1)
                    if isinstance(n, int):
                        dst = t["h1"][a]
                    else:
                        dst = t["h1"][bass.ds(a, 1)].squeeze(0)
                    sp.dma_start(dst, h1[:, :]).then_inc(h1_out, 16)
                if prs:
                    p = b - 1
                    sp.wait_ge(sim16_done, p + 1)
                    sp.dma_start(sim_d, sim16[:, :]).then_inc(sim_out, 16)
                    if att:
                        sp.wait_ge(h1_out, 16 * a + 16)
                    sp.wait_ge(sim_out, 16 * p + 16)
                    at_least(sp, sim_done, p)
                    sp.dma_start(sim_in[:, :].rearrange("i (m j) -> i m j", m=2),
                                 sim_d.rearrange("(m c) (i j) -> (c i) m j", m=2, i=CH)).then_inc(sim_back, 16)
            schedule(sp, step, lambda n, o: None)
            sp.wait_ge(h1_out, 16 * B)

        @block.gpsimd
        def _(pool):
            pool.iota(key_no[:, :], [[1, 1]], base=0, channel_multiplier=1,
                      allow_small_or_imprecise_dtypes=True).then_inc(consts, 1)
            pool.wait_ge(zeros_set, 1)
            pool.wait_ge(consts, 1)
            pool.affine_select(out=ident[:, :], in_=ident[:, :], compare_op=ALU.not_equal, fill=1.0,
                               base=0, pattern=[[-1, 128]], channel_multiplier=1).then_inc(consts, 1)
            pool.affine_select(out=off_diag[:, :], in_=off_diag[:, :], compare_op=ALU.not_equal, fill=0.0,
                               base=0, pattern=[[-1, S]], channel_multiplier=1).then_inc(consts, 1)
            pool.wait_ge(consts, 3)
            pool.affine_select(out=conv_w[CC:, :, 2, CC:], in_=conv_w[CC:, :, 2, CC:], compare_op=ALU.not_equal,
                               fill=1.0, base=0, pattern=[[0, L], [-1, CC]], channel_multiplier=1).then_inc(consts, 1)
            pool.wait_ge(consts, 4)
            pool.wait_ge(w_in, 16 * 37)
            pool.tensor_scalar(bn[:, 5:6], bn[:, 4:5], BN_EPS, None, ALU.add).then_inc(const_chain, 1)
            pool.wait_ge(const_chain, 1)
            pool.tensor_tensor(bn[:, 5:6], bn[:, 5:6], minus_half[:, :], ALU.pow).then_inc(const_chain, 1)

            def step(n, o, tok, prs, att):
                b = 2 * n + o
                if att:
                    a = b - 2
                    pool.wait_ge(sim_back, 16 * a + 16)
                    at_least(pool, idx_done, a)
                    pool.tensor_tensor(sim[:, :], sim_in[:, :], off_diag[:, :], ALU.mult).then_inc(sim_done, 1)
                if tok:
                    for k in range(2):
                        pool.wait_ge(veps_done, 2 * b + k + 1)
                        pool.tensor_tensor(rstd[:, k:k + 1], veps[:, k:k + 1], minus_half[0:S, :],
                                           ALU.pow).then_inc(rstd_done, 1)
            schedule(pool, step, lambda n, o: None)

        @block.tensor
        def _(pe):
            pe.wait_ge(consts, 4)
            pe.wait_ge(w_in, 16 * 37)

            def start(n, o):
                b, e = 2 * n + o, o % 2
                pe.wait_ge(enc_in[e], 16 * (n + o // 2) + 16)
                for q in range(2):
                    mm = pe.matmul(C[:, q * T:q * T + T], cond_w[:, 128 * q:128 * q + 128], enc[:, e, :],
                                   start=True, stop=True)
                mm.then_inc(cond_done, 1)

            def upsample(n, o):
                e = o % 2
                for s in range(2):
                    mm = pe.matmul(Y[:, s * T:s * T + T], up_w[:, s, :], enc[0:CC, e, :], start=True, stop=True)
                mm.then_inc(up_done, 1)

            def layer(l, b, e):
                pe.wait_ge(x_top, 5 * b + l + 1)
                pe.wait_ge(x_bot, 5 * b + l + 1)
                if l == 0:
                    pe.wait_ge(xc_top, L * b + 1)
                for m in range(2):
                    pe.matmul(Y[:, 0:D], conv_w[:, l, m, :], xs[:, 2 * m:2 * m + D], start=(m == 0), stop=False)
                pe.wait_ge(xc_top, L * b + l + 1)
                pe.wait_ge(crep_done, b + 1)
                pe.matmul(Y[:, 0:D], conv_w[:, l, 2, :], xc[:, e, l, :], start=False,
                          stop=True).then_inc(conv_done, 1)

            def step(n, o, tok, prs, att):
                b, p, a = 2 * n + o, 2 * n + o - 1, 2 * n + o - 2
                e = o % 2

                def conv_layer(l):
                    if tok:
                        layer(l, b, e)

                def chunk(c):
                    if not prs:
                        return
                    pe.wait_ge(pair_done, NCH // 2 * p + c // 2 + 1)
                    at_least(pe, r2_done, NCH * p + c - 1)
                    for m in range(2):
                        mm = pe.matmul(Z[c % 2][PG * m:PG * m + PG, 0:CW], w2[:, :],
                                       pair[:, c // 2, CH * (c % 2):CH * (c % 2) + CH, HALF * m:HALF * m + HALF],
                                       start=True, stop=True)
                    mm.then_inc(z_done, 1)
                    if c >= 2:
                        third(c - 2)

                def third(c):
                    if not prs:
                        return
                    pe.wait_ge(r2_done, NCH * p + c + 1)
                    if c == 0:
                        at_least(pe, sim16_done, p)
                    pe.matmul(W[0:16, 0:CW], w3[:, 7 - c:23 - c], r2[:, c % 4, :],
                              start=(c == 0), stop=(c == NCH - 1)).then_inc(w3_done, 1)

                if tok:
                    pe.wait_ge(h_done, b) if prs else None
                    start(n, o + 1)
                if prs:
                    pe.wait_ge(xnT_done, p + 1)
                    for k in range(KD):
                        mm = pe.matmul(X[:, KD * S:KD * S + S], w1[:, k, :], xnT[:, k, :],
                                       start=(k == 0), stop=(k == KD - 1))
                    mm.then_inc(hT_psum, 1)
                    for k in range(KD):
                        mm = pe.matmul(G[0:S, 1, 0:3 * KQ], xnT[:, k, :], wqkv[:, k, :],
                                       start=(k == 0), stop=(k == KD - 1))
                    mm.then_inc(qkv_psum, 1)
                conv_layer(1)
                chunk(0)
                chunk(1)
                chunk(2)
                chunk(3)
                conv_layer(2)
                if att:
                    pe.wait_ge(pick_done, a + 1)
                    pe.wait_ge(qkv_done, (a + 2) if prs else (a + 1))
                    at_least(pe, h1_done, a)
                    for r in range(TOPK):
                        mm = pe.matmul(G[0:S, r // 4, 128 * (r % 4):128 * (r % 4) + 128], pick[:, r, :],
                                       qkv[:, e, KQ:3 * KQ], start=True, stop=True)
                    mm.then_inc(g_done, 1)
                chunk(4)
                conv_layer(3)
                chunk(5)
                chunk(6)
                chunk(7)
                if tok:
                    pe.wait_ge(gated_done, L * b + L)
                    upsample(n, o + 1)
                    pe.wait_ge(x_top, 5 * b + 5)
                    pe.wait_ge(soft_done, b + 2)
                    pe.matmul(C[0:S, 0:D], tok_w[:, :], xs[0:CC, 2:2 + D], start=True, stop=True).then_inc(tok_done, 1)
                if att:
                    pe.wait_ge(ao_done, a + 1)
                    pe.transpose(G[:, 1, 0:S], aon[:, :], ident[0:S, 0:S]).then_inc(aoT_psum, 1)
                third(NCH - 2)
                third(NCH - 1)
                if tok:
                    layer(0, b + 1, 1 - e)
                if att:
                    pe.wait_ge(aoT_done, a + 1)
                    pe.matmul(G[0:S, 0, 0:D], aoT[:, :], wout[:, :], start=True, stop=True).then_inc(wo_done, 1)
                if tok:
                    pe.wait_ge(xn_done, b + 1)
                    for k in range(KD):
                        mm = pe.transpose(X[:, S * k:S * k + S], xn[:, 128 * k:128 * k + 128], ident[0:S, 0:S])
                    mm.then_inc(xnT_psum, 1)
            def first(n, o):
                start(n, o)
                upsample(n, o)
                layer(0, 0, 0)
            schedule(pe, step, first)

        @block.scalar
        def _(act):
            act.wait_ge(w_in, 16 * 37)
            act.wait_ge(bn_ready, 3)

            def absolute(n, o):
                act.wait_ge(cond_done, 2 * n + o + 1)
                act.activation(cabs[:, :], C[:, :], ACT.Abs).then_inc(abs_done, 1)

            def condition(n, o, layers):
                b, e = 2 * n + o, o % 2
                act.wait_ge(soft_done, b + 1)
                for l in layers:
                    q = slice(CC * (l % 2), CC * (l % 2) + CC)
                    ins = act.activation(xc[CC:, e, l, :].rearrange("p (t s) -> p t s", s=2),
                                         soft[q, l // 2, :].unsqueeze(2).to_broadcast([CC, T, 2]),
                                         ACT.Identity, bias=lin_b[q, l // 2:l // 2 + 1])
                if l == L - 1:
                    ins.then_inc(crep_done, 1)

            def upsampled(n, o, part):
                b, e = 2 * n + o, o % 2
                act.wait_ge(up_done, b + 1)
                y = Y[:, :].rearrange("p (s t) -> p t s", s=2)
                dst, q, sig = {"top": (xs[0:CC, 2:2 + D], slice(0, CC), x_top),
                               "bottom": (xs[CC:, 1:1 + D], slice(CC, 2 * CC), x_bot),
                               "fifth": (xc[0:CC, e, 0, 0:D - 2], slice(0, CC), xc_top)}[part]
                y = y[q, 1:, :] if part == "fifth" else y[q, :, :]
                act.activation(dst.rearrange("p (t s) -> p t s", s=2), y, ACT.Relu,
                               bias=up_shift[q, :], scale=up_scale[q, :]).then_inc(sig, 1)

            def step(n, o, tok, prs, att):
                b, p, a = 2 * n + o, 2 * n + o - 1, 2 * n + o - 2
                e = o % 2

                def gate(l):
                    if tok:
                        act.wait_ge(conv_done, L * b + l + 1)
                        act.activation(th[CC:, :], Y[0:CC, 0:D], ACT.Tanh, bias=gate_b[:, l:l + 1],
                                       scale=0.5).then_inc(th_done, 1)

                def top_copy(l):
                    if tok:
                        act.wait_ge(x_bot, 5 * b + l + 2)
                        act.activation(xs[0:CC, 2:2 + D], xs[CC:, 1:1 + D], ACT.Copy).then_inc(x_top, 1)
                        if l + 1 < L:
                            act.activation(xc[0:CC, e, l + 1, 0:D - 2], xs[CC:, 3:1 + D], ACT.Copy).then_inc(xc_top, 1)

                def pair_relu(c):
                    if prs:
                        act.wait_ge(diff_done, NCH // 2 * p + c + 1)
                        act.activation(pair[:, c, :, :], pair[:, c, :, :], ACT.Relu, bias=b1[:, :]).then_inc(pair_done, 1)

                def relu(c):
                    if prs:
                        act.wait_ge(z_done, NCH * p + c + 1)
                        at_least(act, w3_done, NCH * p + c - 3)
                        act.activation(r2[:, c % 4, :], Z[c % 2][:, 0:CW], ACT.Relu, bias=b2[:, :]).then_inc(r2_done, 1)

                def spread(l):
                    if tok:
                        condition(n, o + 1, [l])

                gate(0)
                if tok:
                    absolute(n, o + 1)
                top_copy(0)
                pair_relu(0)
                gate(1)
                pair_relu(1)
                relu(0)
                relu(1)
                top_copy(1)
                relu(2)
                pair_relu(2)
                relu(3)
                gate(2)
                spread(0)
                top_copy(2)
                relu(4)
                pair_relu(3)
                spread(1)
                if att:
                    act.wait_ge(exp_in, a + 1)
                    act.activation(prob[:, :, :], score[:, :, :], ACT.Exp, scale=HD ** -0.5).then_inc(exp_done, 1)
                gate(3)
                relu(5)
                relu(6)
                spread(2)
                top_copy(3)
                relu(7)
                spread(3)
                if tok:
                    act.wait_ge(x_top, 5 * b + 5)
                    upsampled(n, o + 1, "bottom")
                    act.wait_ge(tok_done, b + 1)
                    at_least(act, hx_done, b)
                    act.activation(h[:, :], C[0:S, 0:D], ACT.Identity, bias=tok_b[:, :]).then_inc(h_done, 1)
                    upsampled(n, o + 1, "top")
                if att:
                    act.wait_ge(aoT_psum, a + 1)
                    act.activation(aoT[0:KQ, :], G[0:KQ, 1, 0:S], ACT.Copy).then_inc(aoT_done, 1)
                if prs:
                    act.wait_ge(w3_done, NCH * p + NCH)
                    at_least(act, sim_out, 16 * p)
                    act.activation(sim16[:, :], W[0:16, 0:CW], ACT.Identity, bias=b3[:, :]).then_inc(sim16_done, 1)

            def first(n, o):
                absolute(n, o)
                condition(n, o, range(L))
                for part in ("top", "bottom", "fifth"):
                    upsampled(n, o, part)
            schedule(act, step, first)

        @block.vector
        def _(dve):
            dve.memset(xs[:, :], 0.0)
            dve.memset(xc[0:CC, :, :, D - 2:], 0.0)
            dve.memset(off_diag[:, :], 1.0)
            dve.memset(aon[:, :], 0.0)
            dve.memset(conv_w[CC:, :, 2, :], 0.0)
            dve.memset(w3[:, :], 0.0)
            dve.memset(enc[CC:CC + 1, :, :], 1.0)
            dve.memset(aoT[KQ:KQ + 1, :], 1.0)
            dve.memset(minus_half[:, :], -0.5)
            dve.memset(ident[:, :], 0.0).then_inc(zeros_set, 1)
            dve.wait_ge(w_in, 16 * 37)
            dve.wait_ge(const_chain, 2)
            dve.tensor_scalar(gate_b[:, :], gate_b[:, :], 0.5, None, ALU.mult).then_inc(bn_ready, 1)
            dve.tensor_tensor(up_scale[:, :], bn[:, 1:2], bn[:, 5:6], ALU.mult).then_inc(bn_ready, 1)
            dve.tensor_tensor(up_shift[:, :], bn[:, 0:1], bn[:, 3:4], ALU.subtract).then_inc(const_chain, 1)
            dve.wait_ge(bn_ready, 2)
            dve.wait_ge(const_chain, 3)
            dve.scalar_tensor_tensor(up_shift[:, :], up_shift[:, :], up_scale[:, 0:1], bn[:, 2:3],
                                     ALU.mult, ALU.add).then_inc(bn_ready, 1)

            def recip(n, o, half):
                b = 2 * n + o
                q = slice(T * half, T * half + T)
                if half == 0:
                    dve.wait_ge(abs_done, b + 1)
                    dve.tensor_scalar(cabs[:, :], cabs[:, :], 1.0, None, ALU.add).then_inc(abs1_done, 1)
                    dve.wait_ge(abs1_done, b + 1)
                dve.reciprocal(cabs[:, q], cabs[:, q]).then_inc(recip_done, 1)
                if half == 1:
                    dve.wait_ge(recip_done, 2 * b + 2)
                    at_least(dve, crep_done, b)
                    dve.tensor_tensor(soft[:, :, :].rearrange("p q t -> p (q t)"), C[:, :], cabs[:, :],
                                      ALU.mult).then_inc(soft_done, 1)

            def step(n, o, tok, prs, att):
                b, p, a = 2 * n + o, 2 * n + o - 1, 2 * n + o - 2
                e = o % 2

                def conv_out(l):
                    if not tok:
                        return
                    dve.wait_ge(th_done, L * b + l + 1)
                    dve.scalar_tensor_tensor(gated[CC:, :], th[CC:, :], 1.0, Y[CC:, 0:D],
                                             ALU.add, ALU.mult).then_inc(gated_done, 1)
                    dve.wait_ge(gated_done, L * b + l + 1)
                    dve.scalar_tensor_tensor(xs[CC:, 1:1 + D], gated[CC:, :], 0.5, xs[CC:, 1:1 + D],
                                             ALU.mult, ALU.add).then_inc(x_bot, 1)

                def diff(c, lo=0, hi=GEN):
                    if not prs:
                        return
                    if lo == 0 and c == 0:
                        dve.wait_ge(hT_done, p + 1)
                        at_least(dve, z_done, NCH * p)
                    shape = [128, hi - lo, S]
                    ins = dve.tensor_tensor(pair[:, c, lo:hi, :],
                                            hT[:, GEN * c + lo:GEN * c + hi].unsqueeze(2).to_broadcast(shape),
                                            hT[:, :].unsqueeze(1).to_broadcast(shape), ALU.subtract)
                    if hi == GEN:
                        ins.then_inc(diff_done, 1)

                def stats_of(k, src):
                    dve.bn_stats(stats[:, k, :], src).then_inc(ln_chain, 1)

                def variance(k):
                    dve.bn_aggr(mv[:, k, :], stats[:, k, :]).then_inc(ln_chain, 1)
                    dve.wait_ge(ln_chain, 4 * b + 2 * k + 2)
                    dve.tensor_scalar(veps[:, k:k + 1], mv[:, k, 1:2], LN_EPS, None, ALU.add).then_inc(veps_done, 1)

                conv_out(0)
                if prs:
                    if not tok:
                        dve.wait_ge(h1_done, a)
                    dve.tensor_tensor(hx[:, 1 - e, :], h[:, :], xa[:, :], ALU.add).then_inc(hx_done, 1)
                    dve.wait_ge(hT_psum, p + 1)
                    dve.tensor_copy(hT[:, :], X[:, KD * S:KD * S + S]).then_inc(hT_done, 1)
                    dve.wait_ge(hT_done, p + 1)
                diff(0)
                diff(1)
                if att:
                    dve.wait_ge(sim_done, a + 1)
                if prs:
                    dve.wait_ge(qkv_psum, p + 1)
                    dve.tensor_tensor(qkv[:, (e + 1) % 2, :], G[0:S, 1, 0:3 * KQ], bqkv[:, :],
                                      ALU.add).then_inc(qkv_done, 1)
                if att:
                    if not prs:
                        dve.memset(turn[:, :], 0.0)
                    dve.max(top[:, :], sim[:, :]).then_inc(top_done, 1)
                    dve.wait_ge(top_done, a + 1)
                    dve.memset(turn[:, :], 0.0)
                    dve.max_index(idx[:, :], top[:, :], sim[:, :]).then_inc(idx_done, 1)
                if tok:
                    recip(n, o + 1, 0)
                conv_out(1)
                diff(2)
                if att:
                    dve.wait_ge(idx_back, 16 * a + 16)
                    dve.tensor_scalar(pick[:, :, :], idx_all[:, :, :].rearrange("j i r -> j r i"), key_no[:, 0:1],
                                      None, ALU.is_equal).then_inc(pick_done, 1)
                if tok:
                    recip(n, o + 1, 1)
                conv_out(2)
                diff(3)
                if att:
                    dve.wait_ge(g_done, a + 1)
                    gk = G[0:S, :, :].rearrange("i m (r c) -> i (m r) c", c=2 * KQ)
                    dve.tensor_tensor(prod[:, :, :], gk[:, :, 0:KQ],
                                      qkv[:, e, 0:KQ].unsqueeze(1).to_broadcast([S, TOPK, KQ]),
                                      ALU.mult).then_inc(at_chain, 1)
                    dve.wait_ge(at_chain, 7 * a + 1)
                    pr = prod[:, :, :].rearrange("i r (h d) -> i r h d", d=HD)
                    dve.tensor_tensor(score[:, :, :], pr[:, :, :, 0], pr[:, :, :, 1], ALU.add).then_inc(at_chain, 1)
                    dve.wait_ge(at_chain, 7 * a + 2)
                    dve.tensor_reduce(smax[:, :], score[:, :, :].rearrange("i r h -> i h r"), AX.X,
                                      ALU.max).then_inc(at_chain, 1)
                    dve.wait_ge(at_chain, 7 * a + 3)
                    dve.tensor_tensor(score[:, :, :], score[:, :, :],
                                      smax[:, :].unsqueeze(1).to_broadcast([S, TOPK, NH]),
                                      ALU.subtract).then_inc(exp_in, 1)
                if att:
                    dve.wait_ge(exp_done, a + 1)
                    dve.tensor_reduce(psum_[:, :], prob[:, :, :].rearrange("i r h -> i h r"), AX.X,
                                      ALU.add).then_inc(at_chain, 1)
                    for d in range(HD):
                        ins = dve.tensor_tensor(pv[:, :, :].rearrange("i r (h d) -> i r h d", d=HD)[:, :, :, d],
                                                gk[:, :, KQ:].rearrange("i r (h d) -> i r h d", d=HD)[:, :, :, d],
                                                prob[:, :, :], ALU.mult)
                    ins.then_inc(at_chain, 1)
                conv_out(3)
                if att:
                    dve.wait_ge(at_chain, 7 * a + 4)
                    dve.reciprocal(pinv[:, :], psum_[:, :]).then_inc(at_chain, 1)
                    dve.wait_ge(at_chain, 7 * a + 5)
                    dve.tensor_reduce(ao[:, :], pv[:, :, :].rearrange("i r c -> i c r"), AX.X,
                                      ALU.add).then_inc(at_chain, 1)
                    dve.wait_ge(at_chain, 7 * a + 7)
                    dve.tensor_tensor(aon[:, 0:KQ].rearrange("i (h d) -> i h d", d=HD),
                                      ao[:, :].rearrange("i (h d) -> i h d", d=HD),
                                      pinv[:, :].unsqueeze(2).to_broadcast([S, NH, HD]), ALU.mult).then_inc(ao_done, 1)
                if tok:
                    dve.wait_ge(h_done, b + 1)
                    stats_of(0, h[:, :])
                if tok:
                    dve.wait_ge(ln_chain, 4 * b + 1)
                    dve.memset(turn[:, :], 0.0)
                    variance(0)
                    dve.wait_ge(x_top, 5 * b + 6)
                    dve.tensor_copy(xc[0:CC, 1 - e, 0, 0:D - 2], xs[0:CC, 4:2 + D]).then_inc(xc_top, 1)
                    dve.wait_ge(rstd_done, 2 * b + 1)
                    dve.tensor_scalar(xa[:, :], h[:, :], mv[:, 0, 0:1], rstd[:, 0:1], ALU.subtract,
                                      ALU.mult).then_inc(xa_done, 1)
                    dve.wait_ge(xa_done, b + 1)
                    stats_of(1, xa[:, :])
                    dve.wait_ge(ln_chain, 4 * b + 3)
                    dve.memset(turn[:, :], 0.0)
                    variance(1)
                    dve.wait_ge(rstd_done, 2 * b + 2)
                    at_least(dve, xnT_psum, b)
                    dve.tensor_scalar(xn[:, :], xa[:, :], mv[:, 1, 0:1], rstd[:, 1:2], ALU.subtract,
                                      ALU.mult).then_inc(xn_done, 1)
                    dve.wait_ge(xnT_psum, b + 1)
                    for k in range(KD):
                        ins = dve.tensor_scalar(xnT[:, k, :], X[:, S * k:S * k + S], gamma[:, k:k + 1],
                                                beta[:, k:k + 1], ALU.mult, ALU.add)
                    ins.then_inc(xnT_done, 1)
                if att:
                    dve.wait_ge(wo_done, a + 1)
                    dve.wait_ge(hx_done, a + 1)
                    dve.tensor_tensor(h1[:, :], G[0:S, 0, 0:D], hx[:, e, :], ALU.add).then_inc(h1_done, 1)
            def first(n, o):
                recip(n, o, 0)
                recip(n, o, 1)

            xa_done = sem("xa_done")
            schedule(dve, step, first)


def experts(nc, t):
    N, D = t["h1f"].shape
    KD = D // 128
    E = t["gateT"].shape[1] - 1
    FS = t["sdT"].shape[0]
    I = t["edT"].shape[1]
    NT = 512
    TT = NT // 128
    ST = N // NT
    IH = I // 2
    SF = FS // 128
    with ExitStack() as ctx:
        def sb(name, shape, dt=F32):
            return ctx.enter_context(nc.sbuf_tensor("q_" + name, shape, dt))

        def sem(name):
            return ctx.enter_context(nc.semaphore("q_" + name))
        sg_w = sb("sg_w", [128, KD, FS])
        su_w = sb("su_w", [128, KD, FS])
        sd_w = sb("sd_w", [128, SF, D])
        eg_w = sb("eg_w", [128, KD, E, 2 * I])
        ed_w = sb("ed_w", [IH, E, 2, D])
        rt_w = sb("rt_w", [128, KD, E + 1])
        ident = sb("ident", [128, 128])
        sel = sb("sel", [E + 1, E + 1, 128])
        minus_half = sb("minus_half", [128, TT])
        e_no = sb("e_no", [128, E])
        hin = sb("hin", [128, TT, D])
        xn = sb("xn", [128, TT, D])
        xT = sb("xT", [128, KD, NT])
        stats = sb("stats", [128, TT, 6])
        mv = sb("mv", [128, TT, 2])
        veps = sb("veps", [128, TT])
        rstd = sb("rstd", [128, TT])
        lg = sb("lg", [128, TT, E + 1])
        lmax = sb("lmax", [128, TT])
        pr = sb("pr", [128, TT, E])
        psm = sb("psm", [128, TT])
        top = sb("top", [128, TT, 8])
        idx = sb("idx", [128, TT, 8], U32)
        one = sb("one", [128, 2, TT, E])
        cw = sb("cw", [128, TT, E + 1])
        cwT = sb("cwT", [E + 1, NT])
        cwb = sb("cwb", [128, E + 1, NT])
        nudge = sb("nudge", [128, 1])
        th = sb("th", [128, 2, NT])
        act_ = sb("act_", [128, 2, NT])
        bank = [ctx.enter_context(nc.psum_tensor(f"q_bank{i}", [128, 512], F32)) for i in range(8)]
        GU, OUT = bank[0:4], bank[4:8]

        w_in, consts, zeros = sem("w_in"), sem("consts"), sem("zeros")
        h_in, out_done, out_out = sem("h_in"), sem("out_done"), sem("out_out")
        ln, veps_done, rstd_done, xn_done, xT_psum, xT_done = [sem(x) for x in ("ln", "veps", "rstd", "xn", "xTp", "xTd")]
        lg_psum, rt, exp_in, exp_done, sg_done, cw_done = [sem(x) for x in ("lgp", "rt", "expi", "expd", "sgd", "cwd")]
        cwT_psum, cwT_done, cwb_psum, cwb_done = [sem(x) for x in ("cwTp", "cwTd", "cwbp", "cwbd")]
        gu_done, th_done, a1, act_done, down_done, all_done = [sem(x) for x in ("gu", "th", "a1", "act", "down", "all")]
        block = ctx.enter_context(nc.Block())
        NW = 6
        F = SF + 2 * E
        tiles = [("s", f, 128) for f in range(SF)] + [("e", f, IH) for f in range(2 * E)]

        def schedule(eng, step):
            step(0)
            with eng.Fori(1, ST) as n:
                step(n)

        @block.sync
        def _(sp):
            sp.dma_start(rt_w[:, :, :], t["gateT"].rearrange("(k p) f -> p k f", p=128)).then_inc(w_in, 16)
            sp.dma_start(sg_w[:, :, :], t["sgT"].rearrange("(k p) f -> p k f", p=128)).then_inc(w_in, 16)
            sp.dma_start(su_w[:, :, :], t["suT"].rearrange("(k p) f -> p k f", p=128)).then_inc(w_in, 16)
            sp.dma_start(sd_w[:, :, :], t["sdT"].rearrange("(k p) f -> p k f", p=128)).then_inc(w_in, 16)
            sp.dma_start(eg_w[:, :, :, :].rearrange("p k e f -> p k (e f)"), t["egT"].rearrange("(k p) e f -> p k (e f)", p=128)).then_inc(w_in, 16)
            sp.dma_start(ed_w[:, :, :, :], t["edT"].rearrange("e (h p) d -> p e h d", p=IH)).then_inc(w_in, 16)

            def step(n):
                at_least(sp, out_out, 16 * n)
                src = t["h1f"][n * NT:n * NT + NT] if isinstance(n, int) else t["h1f"][bass.ds(n * NT, NT)]
                dst = t["out"][n * NT:n * NT + NT] if isinstance(n, int) else t["out"][bass.ds(n * NT, NT)]
                sp.dma_start(hin[:, :, :], src.rearrange("(a p) d -> p a d", p=128)).then_inc(h_in, 16)
                sp.wait_ge(out_done, TT * n + TT)
                sp.dma_start(dst.rearrange("(a p) d -> p a d", p=128), hin[:, :, :]).then_inc(out_out, 16)
            schedule(sp, step)
            sp.wait_ge(out_out, 16 * ST)

        @block.gpsimd
        def _(pool):
            pool.iota(e_no[:, :], [[1, E]], base=0, channel_multiplier=0,
                      allow_small_or_imprecise_dtypes=True).then_inc(consts, 1)
            pool.wait_ge(zeros, 1)
            pool.affine_select(out=ident[:, :], in_=ident[:, :], compare_op=ALU.not_equal, fill=1.0,
                               base=0, pattern=[[-1, 128]], channel_multiplier=1).then_inc(consts, 1)
            pool.affine_select(out=sel[:, :, :], in_=sel[:, :, :], compare_op=ALU.not_equal, fill=1.0,
                               base=0, pattern=[[-1, E + 1], [0, 128]], channel_multiplier=1).then_inc(consts, 1)

            def step(n):
                pool.wait_ge(veps_done, n + 1)
                pool.tensor_tensor(rstd[:, :], veps[:, :], minus_half[:, :], ALU.pow).then_inc(rstd_done, 1)
            schedule(pool, step)

        @block.tensor
        def _(pe):
            pe.wait_ge(consts, 3)
            pe.wait_ge(w_in, 16 * NW)

            def down(n, j):
                kind, f, m = tiles[j]
                pe.wait_ge(act_done, F * n + j + 1)
                if j == 0:
                    at_least(pe, out_done, TT * n)
                w = sd_w[:, f, :] if kind == "s" else ed_w[:, f // 2, f % 2, :]
                for a in range(TT):
                    mm = pe.matmul(OUT[a][:, 0:D], act_[0:m, j % 2, 128 * a:128 * a + 128], w,
                                   start=(j == 0), stop=(j == F - 1))
                mm.then_inc(down_done, 1)

            def step(n):
                pe.wait_ge(xn_done, n + 1)
                for k in range(KD):
                    for a in range(TT):
                        mm = pe.transpose(GU[k][:, 128 * a:128 * a + 128], xn[:, a, 128 * k:128 * k + 128], ident[:, :])
                    mm.then_inc(xT_psum, 1)
                pe.wait_ge(xT_done, KD * n + KD)
                for a in range(TT):
                    for k in range(KD):
                        mm = pe.matmul(GU[0][:, 16 * a:16 * a + E + 1], xT[:, k, 128 * a:128 * a + 128], rt_w[:, k, :],
                                       start=(k == 0), stop=(k == KD - 1))
                mm.then_inc(lg_psum, 1)
                pe.wait_ge(cw_done, 2 * n + 2)
                for a in range(TT):
                    mm = pe.transpose(GU[1][0:E + 1, 128 * a:128 * a + 128], cw[:, a, :], ident[:, :])
                mm.then_inc(cwT_psum, 1)
                pe.wait_ge(cwT_done, n + 1)
                for q in range(E + 1):
                    at_least(pe, cwb_done, (E + 1) * n + q - 1)
                    pe.matmul(GU[2 + q % 2][:, :], sel[:, q, :], cwT[:, :], start=True, stop=True).then_inc(cwb_psum, 1)
                pe.wait_ge(cwb_done, (E + 1) * n + E + 1)
                for j, (kind, f, m) in enumerate(tiles):
                    if j >= 2:
                        pe.wait_ge(act_done, F * n + j - 1)
                    for h in range(2):
                        for k in range(KD):
                            if kind == "s":
                                w = (su_w if h else sg_w)[:, k, 128 * f:128 * f + 128]
                            else:
                                c = I * h + IH * (f % 2)
                                w = eg_w[:, k, f // 2, c:c + IH]
                            mm = pe.matmul(GU[2 * (j % 2) + h][0:m, :], w, xT[:, k, :], start=(k == 0), stop=(k == KD - 1))
                        mm.then_inc(gu_done, 1)
                    if j:
                        down(n, j - 1)
                down(n, F - 1)
            schedule(pe, step)

        @block.scalar
        def _(act):
            def step(n):
                for k in range(KD):
                    act.wait_ge(xT_psum, KD * n + k + 1)
                    act.activation(xT[:, k, :], GU[k][:, :], ACT.Copy).then_inc(xT_done, 1)
                act.wait_ge(lg_psum, n + 1)
                act.activation(lg[:, :, :], GU[0][:, 0:16 * TT].rearrange("p (a e) -> p a e", e=16)[:, :, 0:E + 1], ACT.Copy).then_inc(rt, 1)
                act.wait_ge(exp_in, n + 1)
                act.activation(pr[:, :, :], pr[:, :, :], ACT.Exp).then_inc(exp_done, 1)
                act.activation(cw[:, :, E:E + 1], lg[:, :, E:E + 1], ACT.Tanh, scale=0.5).then_inc(sg_done, 1)
                act.wait_ge(cwT_psum, n + 1)
                act.activation(cwT[:, :], GU[1][0:E + 1, :], ACT.Copy, scale=0.5).then_inc(cwT_done, 1)
                for q in range(E + 1):
                    act.wait_ge(cwb_psum, (E + 1) * n + q + 1)
                    act.activation(cwb[:, q, :], GU[2 + q % 2][:, :], ACT.Copy).then_inc(cwb_done, 1)
                for j, (kind, f, m) in enumerate(tiles):
                    act.wait_ge(gu_done, 2 * (F * n + j) + 1)
                    at_least(act, act_done, F * n + j - 1)
                    act.activation(th[0:m, j % 2, :], GU[2 * (j % 2)][0:m, :], ACT.Tanh, scale=0.5).then_inc(th_done, 1)
            schedule(act, step)

        @block.vector
        def _(dve):
            dve.memset(ident[:, :], 0.0)
            dve.memset(minus_half[:, :], -0.5)
            dve.memset(sel[:, :, :], 0.0).then_inc(zeros, 1)

            def chain(s, n, k, per):
                dve.wait_ge(s, per * n + k)

            def step(n):
                dve.wait_ge(h_in, 16 * n + 16)
                for a in range(TT):
                    dve.bn_stats(stats[:, a, :], hin[:, a, :]).then_inc(ln, 1)
                dve.wait_ge(ln, 2 * TT * n + TT)
                dve.memset(nudge[:, :], 0.0)
                for a in range(TT):
                    dve.bn_aggr(mv[:, a, :], stats[:, a, :]).then_inc(ln, 1)
                dve.wait_ge(ln, 2 * TT * n + 2 * TT)
                dve.tensor_scalar(veps[:, :], mv[:, :, 1], LN_EPS, None, ALU.add).then_inc(veps_done, 1)
                dve.wait_ge(rstd_done, n + 1)
                for a in range(TT):
                    ins = dve.tensor_scalar(xn[:, a, :], hin[:, a, :], mv[:, a, 0:1], rstd[:, a:a + 1],
                                            ALU.subtract, ALU.mult)
                ins.then_inc(xn_done, 1)
                dve.wait_ge(rt, n + 1)
                dve.tensor_reduce(lmax[:, :], lg[:, :, 0:E], AX.X, ALU.max).then_inc(a1, 1)
                K = 8 + F * 2
                dve.wait_ge(a1, K * n + 1)
                dve.tensor_tensor(pr[:, :, :], lg[:, :, 0:E], lmax[:, :].unsqueeze(2).to_broadcast([128, TT, E]),
                                  ALU.subtract).then_inc(exp_in, 1)
                dve.wait_ge(exp_done, n + 1)
                dve.tensor_reduce(psm[:, :], pr[:, :, :], AX.X, ALU.add).then_inc(a1, 1)
                dve.wait_ge(a1, K * n + 2)
                dve.reciprocal(psm[:, :], psm[:, :]).then_inc(a1, 1)
                dve.wait_ge(a1, K * n + 3)
                dve.tensor_tensor(pr[:, :, :], pr[:, :, :], psm[:, :].unsqueeze(2).to_broadcast([128, TT, E]),
                                  ALU.mult).then_inc(a1, 1)
                dve.wait_ge(a1, K * n + 4)
                dve.memset(nudge[:, :], 0.0)
                for a in range(TT):
                    ins = dve.max(top[:, a, :], pr[:, a, :])
                ins.then_inc(a1, 1)
                dve.wait_ge(a1, K * n + 5)
                dve.memset(nudge[:, :], 0.0)
                for a in range(TT):
                    ins = dve.max_index(idx[:, a, :], top[:, a, :], pr[:, a, :])
                ins.then_inc(a1, 1)
                dve.tensor_tensor(psm[:, :], top[:, :, 0], top[:, :, 1], ALU.add).then_inc(a1, 1)
                dve.wait_ge(a1, K * n + 7)
                dve.reciprocal(psm[:, :], psm[:, :])
                for k in range(2):
                    ins = dve.tensor_tensor(one[:, k, :, :], e_no[:, :].unsqueeze(1).to_broadcast([128, TT, E]),
                                            idx[:, :, k:k + 1].to_broadcast([128, TT, E]), ALU.is_equal)
                ins.then_inc(a1, 1)
                dve.wait_ge(a1, K * n + 8)
                dve.tensor_tensor(one[:, 0, :, :], one[:, 0, :, :], one[:, 1, :, :], ALU.add).then_inc(r2, 1)
                dve.tensor_tensor(pr[:, :, :], pr[:, :, :], psm[:, :].unsqueeze(2).to_broadcast([128, TT, E]),
                                  ALU.mult).then_inc(r2, 1)
                dve.wait_ge(r2, 2 * n + 2)
                dve.tensor_tensor(cw[:, :, 0:E], pr[:, :, :], one[:, 0, :, :], ALU.mult).then_inc(cw_done, 1)
                dve.wait_ge(sg_done, n + 1)
                dve.tensor_scalar(cw[:, :, E:E + 1], cw[:, :, E:E + 1], 1.0, 0.5, ALU.add, ALU.mult).then_inc(cw_done, 1)
                for j, (kind, f, m) in enumerate(tiles):
                    q = E if kind == "s" else f // 2
                    dve.wait_ge(th_done, F * n + j + 1)
                    at_least(dve, down_done, F * n + j - 1)
                    x = act_[0:m, j % 2, :]
                    dve.scalar_tensor_tensor(x, th[0:m, j % 2, :], 1.0, GU[2 * (j % 2)][0:m, :], ALU.add,
                                             ALU.mult).then_inc(a1, 1)
                    dve.wait_ge(a1, K * n + 9 + 2 * j)
                    dve.wait_ge(gu_done, 2 * (F * n + j) + 2)
                    dve.tensor_tensor(x, x, GU[2 * (j % 2) + 1][0:m, :], ALU.mult).then_inc(a1, 1)
                    dve.wait_ge(a1, K * n + 10 + 2 * j)
                    dve.tensor_tensor(x, x, cwb[0:m, q, :], ALU.mult).then_inc(act_done, 1)
                dve.wait_ge(down_done, F * n + F)
                for a in range(TT):
                    dve.tensor_tensor(hin[:, a, :], OUT[a][:, :], hin[:, a, :], ALU.add).then_inc(out_done, 1)
            r2 = sem("r2")
            schedule(dve, step)


def program(nc, t):
    B, S, D = t["out"].shape
    scratch = nc.dram_tensor("h1_d", (B, S, D), F32, kind="Internal").ap()
    t["h1"] = scratch
    t["h1f"] = scratch.rearrange("b s d -> (b s) d")
    tokens_and_attention(nc, t)
    t["out"] = t["out"].rearrange("b s d -> (b s) d")
    experts(nc, t)


def kernel(**inputs):
    import numpy as np
    import concourse.bacc as bacc
    from concourse.bass_utils import run_bass_kernel_spmd as run

    i = {k: np.asarray(v) for k, v in inputs.items()}
    tok = {k[7:]: v for k, v in i.items() if k.startswith("L0_tok_")}
    att = {k[8:]: v for k, v in i.items() if k.startswith("L0_attn_")}
    ffn = {k[7:]: v for k, v in i.items() if k.startswith("L0_ffn_")}
    x = i["x"].transpose(0, 2, 1)
    CI = tok["up_b"].shape[0]
    D, L = att["gamma"].shape[0], tok["conv_bs"].shape[0]

    def col(a):
        return a.reshape(-1, 1)

    laid = {
        "xT": np.concatenate([x, x[:2]]),
        "up_wT": tok["up_w"].transpose(0, 2, 1),
        "convT": tok["conv_ws"].transpose(3, 2, 0, 1),
        "gate_b": tok["conv_bs"][:, :CI].T,
        "lin_b": tok["conv_bs"][:, CI:].reshape(L // 2, 2, CI).transpose(1, 2, 0).reshape(2 * CI, L // 2),
        "condT": tok["cond_ws"].transpose(2, 0, 1).reshape(-1, L * CI),
        "cond_b": tok["cond_bs"].reshape(1, L * CI),
        "out_wT": tok["out_w"].T,
        "out_b": col(tok["out_b"]),
        "up_b": col(tok["up_b"]),
        "bn_gamma": col(tok["bn_gamma"]),
        "bn_beta": col(tok["bn_beta"]),
        "bn_mean": col(tok["bn_mean"]),
        "bn_var": col(tok["bn_var"]),
        "gamma": att["gamma"].reshape(D // 128, 128).T,
        "beta": att["beta"].reshape(D // 128, 128).T,
        "W1T": att["W1"].T,
        "b1": col(att["b1"]),
        "W2T": att["W2"].T,
        "b2": col(att["b2"]),
        "W3T": att["W3"].T,
        "b3": att["b3"],
        "WqkvT": att["Wqkv"].T,
        "bqkv": att["bqkv"],
        "WoutT": att["Wout"].T,
        "bout": att["bout"].reshape(1, D),
        "gateT": np.concatenate([ffn["gate_w"], ffn["shared_expert_gate_w"]]).T,
        "sgT": ffn["shared_gate_w"].T,
        "suT": ffn["shared_up_w"].T,
        "sdT": ffn["shared_down_w"].T,
        "egT": ffn["gate_up_proj"].transpose(2, 0, 1),
        "edT": ffn["down_proj"].transpose(0, 2, 1),
    }
    nc = bacc.Bacc("TRN2", target_bir_lowering=False, num_devices=1)
    arrays, t = {}, {}
    for name, a in laid.items():
        a = np.ascontiguousarray(a)
        arrays[f"in_{name}"] = a
        t[name] = nc.dram_tensor(f"in_{name}", a.shape, mybir.dt.from_np(a.dtype), kind="ExternalInput").ap()
    shape = (x.shape[0], tok["out_b"].shape[0], 2 * x.shape[2])
    t["out"] = nc.dram_tensor("out_0", shape, F32, kind="ExternalOutput").ap()
    program(nc, t)
    r = run(nc, [arrays], core_ids=[0])
    return r.results[0]["out_0"]
```

```python
import concourse.bass as bass
from concourse import mybir
from contextlib import ExitStack

F32 = mybir.dt.float32
F32R = mybir.dt.float32r
U32 = mybir.dt.uint32
I32 = mybir.dt.int32
ALU = mybir.AluOpType
ACT = mybir.ActivationFunctionType
AX = mybir.AxisListType

BN_EPS = 1e-5
LN_EPS = 1e-5
TOPK = 8


def vector_columns(layers, blocks):
    sizes = dict(up_b=1, bn_gamma=1, bn_beta=1, bn_mean=1, bn_var=1, gate_b=layers, lin_b=2, tok_b=1,
                 gamma=blocks, beta=blocks, b1=1, b2=1, b3=1)
    at, columns = 0, {}
    for name, size in sizes.items():
        columns[name] = slice(at, at + size)
        at += size
    return columns, at


def at_least(eng, sem, value):
    if isinstance(value, int) and value <= 0:
        return
    eng.wait_ge(sem, value)


def tokens_and_attention(nc, t, later=()):
    B, CC, T = t["xT"].shape[0] - 2, *t["xT"].shape[1:]
    L, S = t["conv_w"].shape[1], t["tok_w"].shape[1]
    D = 2 * T
    KD = D // 128
    HF = t["W1T"].shape[1]
    PG = t["W2T"].shape[1]
    KQ = t["wout"].shape[0] - 1
    HD = 2
    NH = KQ // HD
    PAD = D + 4
    CH = 10
    NCH = S // CH
    HALF = S // 2
    CW = CH * HALF

    with ExitStack() as ctx:
        def sb(name, shape, dt=F32):
            return ctx.enter_context(nc.sbuf_tensor(name, shape, dt))

        def ps(name, shape):
            return ctx.enter_context(nc.psum_tensor(name, shape, F32))

        def sem(name):
            return ctx.enter_context(nc.semaphore(name))

        up_w = sb("up_w", [CC, 2, 2 * CC])
        columns, width = vector_columns(L, KD)
        vectors = sb("vectors", [128, width])
        up_b, bn_gamma, bn_beta, bn_mean, bn_var = [
            vectors[:, columns[k]] for k in ("up_b", "bn_gamma", "bn_beta", "bn_mean", "bn_var")]
        gate_bias, lin_b = vectors[0:64, columns["gate_b"]], vectors[:, columns["lin_b"]]
        tok_b, gamma, beta = vectors[0:S, columns["tok_b"]], vectors[:, columns["gamma"]], vectors[:, columns["beta"]]
        b1, b2, b3 = [vectors[:, columns[k]] for k in ("b1", "b2", "b3")]
        bn_rstd = sb("bn_rstd", [128, 1])
        up_scale = sb("up_scale", [128, 1])
        up_shift = sb("up_shift", [128, 1])
        conv_w = sb("conv_w", [128, L, 3, 128])
        gate_b = sb("gate_b", [64, L])
        cond_w = sb("cond_w", [CC + 1, L * CC])
        tok_w = sb("tok_w", [CC, S])
        w1 = sb("w1", [128, KD, HF])
        w2 = sb("w2", [128, PG])
        w3 = sb("w3", [128, 34])
        wqkv = sb("wqkv", [128, KD, 3 * KQ])
        bqkv = sb("bqkv", [S, 3 * KQ])
        wout = sb("wout", [KQ + 1, D])
        ident = sb("ident", [128, 128])
        key_no = sb("key_no", [S, 1])
        off_diag = sb("off_diag", [S, S])
        minus_half = sb("minus_half", [128, 1])

        enc = sb("enc", [CC + 1, 2, T])
        xs = sb("xs", [128, PAD])
        cabs = sb("cabs", [128, 2 * T])
        soft = sb("soft", [128, 2, T])
        xc = sb("xc", [128, 2, L, D])
        th = sb("th", [128, D])
        gated = sb("gated", [128, D])
        h = sb("h", [S, D])
        xa = sb("xa", [S, D])
        hx = sb("hx", [S, 2, D])
        xn = sb("xn", [S, D])
        stats = sb("stats", [S, 2, 6])
        mv = sb("mv", [S, 2, 2])
        turn = sb("turn", [1, 1])
        veps = sb("veps", [S, 2])
        rstd = sb("rstd", [S, 2])
        xnT = sb("xnT", [128, KD, S])
        hT = sb("hT", [128, S])
        pair = sb("pair", [128, NCH, CH, S])
        r2 = sb("r2", [128, NCH, CW])
        sim_rows = sb("sim_rows", [128, CW])
        qkv = sb("qkv", [S, 2, 3 * KQ])
        sim_in = sb("sim_in", [S, S])
        sim = sb("sim", [S, S])
        top = sb("top", [S, TOPK])
        idx = sb("idx", [S, TOPK], U32)
        idx_all = sb("idx_all", [S, S, TOPK], U32)
        pick = sb("pick", [S, TOPK, S])
        prod = sb("prod", [S, TOPK, KQ])
        score = sb("score", [S, TOPK, NH])
        smax = sb("smax", [S, NH])
        prob = sb("prob", [S, TOPK, NH])
        psum_ = sb("psum_", [S, NH])
        pinv = sb("pinv", [S, NH])
        pv = sb("pv", [S, TOPK, KQ])
        ao = sb("ao", [S, KQ])
        aon = sb("aon", [S, 128])
        aoT = sb("aoT", [KQ + 1, S])
        h1 = sb("h1", [S, D])

        Y = ps("Y", [128, 512])
        C = ps("C", [128, 512])
        Z = [ps("Z0", [128, 512]), ps("Z1", [128, 512])]
        W = ps("W", [128, 512])
        G = ps("G", [128, 2, 512])
        X = ps("X", [128, 512])

        sim_d = nc.dram_tensor("sim_d", (128, CW), F32, kind="Internal").ap()
        idx_d = nc.dram_tensor("idx_d", (S, TOPK), U32, kind="Internal").ap()

        tok_w_in, att_w_in, later_in = sem("tok_w_in"), sem("att_w_in"), sem("later_in")
        consts = sem("consts")
        zeros_set = sem("zeros_set")
        const_chain = sem("const_chain")
        bn_ready = sem("bn_ready")
        enc_in = [sem("enc_in0"), sem("enc_in1")]
        up_done, cond_done, conv_done, tok_done = sem("up_done"), sem("cond_done"), sem("conv_done"), sem("tok_done")
        x_top, x_bot, xc_top, crep_done = sem("x_top"), sem("x_bot"), sem("xc_top"), sem("crep_done")
        abs_done, abs1_done, recip_done, soft_done = sem("abs_done"), sem("abs1_done"), sem("recip_done"), sem("soft_done")
        th_done, gated_done = sem("th_done"), sem("gated_done")
        h_done, ln_chain, veps_done, rstd_done = sem("h_done"), sem("ln_chain"), sem("veps_done"), sem("rstd_done")
        xa_done, xn_done, hx_done = sem("xa_done"), sem("xn_done"), sem("hx_done")
        xnT_psum, xnT_done, hT_psum, hT_done = sem("xnT_psum"), sem("xnT_done"), sem("hT_psum"), sem("hT_done")
        qkv_psum, qkv_done = sem("qkv_psum"), sem("qkv_done")
        diff_done, pair_done, z_done, r2_done, w3_done = sem("diff_done"), sem("pair_done"), sem("z_done"), sem("r2_done"), sem("w3_done")
        sim_rows_done, sim_out, sim_back, sim_done = sem("sim_rows_done"), sem("sim_out"), sem("sim_back"), sem("sim_done")
        top_done, idx_done, idx_out, idx_back = sem("top_done"), sem("idx_done"), sem("idx_out"), sem("idx_back")
        pick_done, g_done = sem("pick_done"), sem("g_done")
        at_chain, exp_in, exp_done, ao_done = sem("at_chain"), sem("exp_in"), sem("exp_done"), sem("ao_done")
        aoT_psum, aoT_done, wo_done = sem("aoT_psum"), sem("aoT_done"), sem("wo_done")
        h1_done = sem("h1_done")
        h1_free = sem("h1_free")

        block = ctx.enter_context(nc.Block())

        def schedule(eng, step, start):
            start(0, 0)
            step(0, 0, True, False, False)
            step(0, 1, True, True, False)
            with eng.Fori(1, B // 2) as n:
                step(n, 0, True, True, True)
                step(n, 1, True, True, True)
            step(B // 2, 0, False, True, True)
            step(B // 2, 1, False, False, True)

        @block.sync
        def _(sp):
            sp.wait_ge(zeros_set, 1)
            for k in range(2):
                sp.dma_start(enc[0:CC, k, :], t["xT"][k]).then_inc(enc_in[k], 16)
            for dst, src in [(cond_w[:, :], t["cond_w"]), (up_w[:, :, :], t["up_w"]), (vectors[:, :], t["vectors"]),
                             (conv_w[:, :, :, :], t["conv_w"]), (tok_w[:, :], t["tok_w"])]:
                sp.dma_start(dst, src).then_inc(tok_w_in, 16)
            for dst, src in [(w1[:, :, :], t["W1T"].rearrange("(k p) f -> p k f", p=128)),
                             (w2[:, :], t["W2T"]), (w3[:, :], t["w3"]),
                             (wqkv[:, :, :], t["WqkvT"].rearrange("(k p) f -> p k f", p=128)),
                             (bqkv[:, :], t["bqkv"].partition_broadcast(S)), (wout[:, :], t["wout"])]:
                sp.dma_start(dst, src).then_inc(att_w_in, 16)
            for dst, src in later:
                sp.dma_start(dst, src).then_inc(later_in, 16)

            def step(n, o, tok, prs, att):
                b = 2 * n + o
                if tok:
                    sp.wait_ge(up_done, b + 1)
                    sp.wait_ge(cond_done, b + 1)
                    src = t["xT"][b + 2] if isinstance(n, int) else t["xT"][bass.ds(b + 2, 1)].squeeze(0)
                    sp.dma_start(enc[0:CC, o % 2, :], src).then_inc(enc_in[o % 2], 16)
                if att:
                    a = b - 2
                    sp.wait_ge(idx_done, a + 1)
                    sp.dma_start(idx_d, idx[:, :]).then_inc(idx_out, 16)
                    sp.wait_ge(idx_out, 16 * a + 16)
                    sp.dma_start(idx_all[:, :, :], idx_d.partition_broadcast(S)).then_inc(idx_back, 16)
                if prs:
                    p = b - 1
                    sp.wait_ge(sim_rows_done, p + 1)
                    sp.dma_start(sim_d, sim_rows[:, :]).then_inc(sim_out, 16)
                    sp.wait_ge(sim_out, 16 * p + 16)
                    at_least(sp, sim_done, p)
                    for s in range(2):
                        for m in range(2):
                            sp.dma_start(sim_in[HALF * s:HALF * s + HALF, HALF * m:HALF * m + HALF],
                                         sim_d.rearrange("(g r) (i j) -> r g i j", g=4, i=CH)[2 * s + m]
                                         ).then_inc(sim_back, 16)
                if att:
                    sp.wait_ge(h1_done, a + 1)
                    dst = t["h1"][a] if isinstance(n, int) else t["h1"][bass.ds(a, 1)].squeeze(0)
                    sp.dma_start(dst, h1[:, :]).then_inc(h1_free, 16)
            schedule(sp, step, lambda n, o: None)
            sp.wait_ge(h1_free, 16 * B + 16)
            if later:
                sp.wait_ge(later_in, 16 * len(later))

        @block.gpsimd
        def _(pool):
            pool.iota(key_no[:, :], [[1, 1]], base=0, channel_multiplier=1,
                      allow_small_or_imprecise_dtypes=True).then_inc(consts, 1)
            pool.wait_ge(zeros_set, 1)
            pool.wait_ge(consts, 1)
            pool.affine_select(out=ident[:, :], in_=ident[:, :], compare_op=ALU.not_equal, fill=1.0,
                               base=0, pattern=[[-1, 128]], channel_multiplier=1).then_inc(consts, 1)
            pool.affine_select(out=off_diag[:, :], in_=off_diag[:, :], compare_op=ALU.not_equal, fill=0.0,
                               base=0, pattern=[[-1, S]], channel_multiplier=1).then_inc(consts, 1)
            pool.wait_ge(tok_w_in, 16 * 5)
            pool.tensor_scalar(bn_rstd[:, :], bn_var, BN_EPS, None, ALU.add).then_inc(const_chain, 1)
            pool.wait_ge(const_chain, 1)
            pool.tensor_tensor(bn_rstd[:, :], bn_rstd[:, :], minus_half[:, :], ALU.pow).then_inc(const_chain, 1)

            def step(n, o, tok, prs, att):
                b, e = 2 * n + o, o % 2
                if att:
                    a = b - 2
                    pool.wait_ge(sim_back, 64 * a + 64)
                    if not tok:
                        pool.wait_ge(idx_done, a)
                    pool.tensor_tensor(sim[:, :], sim_in[:, :], off_diag[:, :], ALU.mult).then_inc(sim_done, 1)
                if prs:
                    pool.wait_ge(diff_done, NCH * (b - 1) + 1)
                    pool.tensor_tensor(hx[:, 1 - e, :], h[:, :], xa[:, :], ALU.add).then_inc(hx_done, 1)
                if tok:
                    for k in range(2):
                        pool.wait_ge(veps_done, 2 * b + k + 1)
                        pool.tensor_tensor(rstd[:, k:k + 1], veps[:, k:k + 1], minus_half[0:S, :],
                                           ALU.pow).then_inc(rstd_done, 1)
            schedule(pool, step, lambda n, o: None)

        @block.tensor
        def _(pe):
            pe.wait_ge(consts, 3)
            pe.wait_ge(tok_w_in, 16 * 5)

            def start(n, o):
                b, e = 2 * n + o, o % 2
                pe.wait_ge(enc_in[e], 16 * (n + o // 2) + 16)
                for q in range(2):
                    mm = pe.matmul(C[:, q * T:q * T + T], cond_w[:, 128 * q:128 * q + 128], enc[:, e, :],
                                   start=True, stop=True)
                mm.then_inc(cond_done, 1)

            def upsample(n, o):
                e = o % 2
                for s in range(2):
                    mm = pe.matmul(Y[:, s * T:s * T + T], up_w[:, s, :], enc[0:CC, e, :], start=True, stop=True)
                mm.then_inc(up_done, 1)

            def layer(l, b, e, between=None):
                pe.wait_ge(x_top, 5 * b + l + 1)
                pe.wait_ge(x_bot, 5 * b + l + 1)
                if l == 0:
                    pe.wait_ge(xc_top, L * b + 1)
                for m in range(2):
                    pe.matmul(Y[:, 0:D], conv_w[:, l, m, :], xs[:, 2 * m:2 * m + D], start=(m == 0), stop=False)
                if between:
                    between()
                pe.wait_ge(xc_top, L * b + l + 1)
                pe.wait_ge(crep_done, L * b + l + 1)
                pe.matmul(Y[:, 0:D], conv_w[:, l, 2, :], xc[:, e, l, :], start=False,
                          stop=True).then_inc(conv_done, 1)

            def step(n, o, tok, prs, att):
                b, p, a = 2 * n + o, 2 * n + o - 1, 2 * n + o - 2
                e = o % 2

                def conv_layer(l):
                    if tok:
                        layer(l, b, e)

                def turn():
                    pe.wait_ge(xn_done, b + 1)
                    for k in range(KD):
                        mm = pe.transpose(X[:, S * k:S * k + S], xn[:, 128 * k:128 * k + 128], ident[0:S, 0:S])
                    mm.then_inc(xnT_psum, 1)

                def chunk(c):
                    if not prs:
                        return
                    pe.wait_ge(pair_done, NCH * p + c + 1)
                    at_least(pe, r2_done, NCH * p + c - 1)
                    for m in range(2):
                        mm = pe.matmul(Z[c % 2][PG * m:PG * m + PG, 0:CW], w2[:, :],
                                       pair[:, c, :, HALF * m:HALF * m + HALF],
                                       start=True, stop=True)
                    mm.then_inc(z_done, 1)

                def third(s):
                    if not prs:
                        return
                    pe.wait_ge(r2_done, NCH * p + 4 * s + 4)
                    if s == 0:
                        at_least(pe, sim_rows_done, p)
                    for g in range(4):
                        mm = pe.matmul(W[32 * g:32 * g + 32, 0:CW], w3[:, 2 - 2 * s:34 - 2 * s], r2[:, 4 * s + g, :],
                                       start=(s == 0), stop=(s == 1))
                    mm.then_inc(w3_done, 1)

                if prs:
                    pe.wait_ge(xnT_done, p + 1)
                    for k in range(KD):
                        mm = pe.matmul(X[:, KD * S:KD * S + S], w1[:, k, :], xnT[:, k, :],
                                       start=(k == 0), stop=(k == KD - 1))
                    mm.then_inc(hT_psum, 1)
                    for k in range(KD):
                        mm = pe.matmul(G[0:S, 1, 0:3 * KQ], xnT[:, k, :], wqkv[:, k, :],
                                       start=(k == 0), stop=(k == KD - 1))
                    mm.then_inc(qkv_psum, 1)
                conv_layer(1)
                chunk(0)
                chunk(1)
                chunk(2)
                chunk(3)
                conv_layer(2)
                third(0)
                if att:
                    pe.wait_ge(pick_done, a + 1)
                    pe.wait_ge(qkv_done, (a + 2) if prs else (a + 1))
                    if not prs:
                        pe.wait_ge(h1_done, a)
                    for r in range(TOPK):
                        mm = pe.matmul(G[0:S, r // 4, 128 * (r % 4):128 * (r % 4) + 128], pick[:, r, :],
                                       qkv[:, e, KQ:3 * KQ], start=True, stop=True)
                    mm.then_inc(g_done, 1)
                chunk(4)
                conv_layer(3)
                chunk(5)
                chunk(6)
                if tok:
                    pe.wait_ge(gated_done, L * b + L)
                    upsample(n, o + 1)
                    pe.wait_ge(x_top, 5 * b + 5)
                    pe.wait_ge(soft_done, b + 2)
                    pe.matmul(C[0:S, 0:D], tok_w[:, :], xs[0:CC, 2:2 + D], start=True, stop=True).then_inc(tok_done, 1)
                chunk(7)
                if att:
                    pe.wait_ge(ao_done, a + 1)
                    pe.transpose(G[:, 1, 0:S], aon[:, :], ident[0:S, 0:S]).then_inc(aoT_psum, 1)
                if tok:
                    pe.wait_ge(h_done, b + 1)
                    start(n, o + 2)
                third(1)
                if tok:
                    layer(0, b + 1, 1 - e, turn)
                if att:
                    pe.wait_ge(aoT_done, a + 1)
                    pe.matmul(G[0:S, 0, 0:D], aoT[:, :], wout[:, :], start=True, stop=True).then_inc(wo_done, 1)

            def first(n, o):
                start(n, o)
                upsample(n, o)
                layer(0, 0, 0)
                pe.wait_ge(soft_done, 1)
                start(n, o + 1)
                pe.wait_ge(att_w_in, 16 * 6)
            schedule(pe, step, first)

        @block.scalar
        def _(act):
            act.wait_ge(tok_w_in, 16 * 5)
            act.wait_ge(bn_ready, 3)

            def absolute(n, o):
                act.wait_ge(cond_done, 2 * n + o + 1)
                act.activation(cabs[:, :], C[:, :], ACT.Abs).then_inc(abs_done, 1)

            def condition(n, o, layers):
                b, e = 2 * n + o, o % 2
                act.wait_ge(soft_done, b + 1)
                for l in layers:
                    q = slice(CC * (l % 2), CC * (l % 2) + CC)
                    act.activation(xc[CC:, e, l, :].rearrange("p (t s) -> p t s", s=2),
                                   soft[q, l // 2, :].unsqueeze(2).to_broadcast([CC, T, 2]),
                                   ACT.Identity, bias=lin_b[q, l // 2:l // 2 + 1]).then_inc(crep_done, 1)

            def upsampled(n, o, part):
                b, e = 2 * n + o, o % 2
                act.wait_ge(up_done, b + 1)
                y = Y[:, :].rearrange("p (s t) -> p t s", s=2)
                dst, q, sig = {"top": (xs[0:CC, 2:2 + D], slice(0, CC), x_top),
                               "bottom": (xs[CC:, 1:1 + D], slice(CC, 2 * CC), x_bot),
                               "fifth": (xc[0:CC, e, 0, 0:D - 2], slice(0, CC), xc_top)}[part]
                y = y[q, 1:, :] if part == "fifth" else y[q, :, :]
                act.activation(dst.rearrange("p (t s) -> p t s", s=2), y, ACT.Relu,
                               bias=up_shift[q, :], scale=up_scale[q, :]).then_inc(sig, 1)

            def step(n, o, tok, prs, att):
                b, p, a = 2 * n + o, 2 * n + o - 1, 2 * n + o - 2
                e = o % 2

                def gate(l):
                    if tok:
                        act.wait_ge(conv_done, L * b + l + 1)
                        act.activation(th[CC:, :], Y[0:CC, 0:D], ACT.Tanh, bias=gate_b[:, l:l + 1],
                                       scale=0.5).then_inc(th_done, 1)

                def top_copy(l):
                    if tok:
                        act.wait_ge(x_bot, 5 * b + l + 2)
                        act.activation(xs[0:CC, 2:2 + D], xs[CC:, 1:1 + D], ACT.Copy).then_inc(x_top, 1)
                        if l + 1 < L:
                            act.activation(xc[0:CC, e, l + 1, 0:D - 2], xs[CC:, 3:1 + D], ACT.Copy).then_inc(xc_top, 1)

                def pair_relu(lo, hi):
                    if prs:
                        act.wait_ge(diff_done, NCH * p + hi)
                        act.activation(pair[:, lo:hi, :, :], pair[:, lo:hi, :, :], ACT.Relu,
                                       bias=b1).then_inc(pair_done, hi - lo)

                def relu(c):
                    if prs:
                        act.wait_ge(z_done, NCH * p + c + 1)
                        at_least(act, w3_done, 2 * p - 1 + c // 4)
                        act.activation(r2[:, c, :], Z[c % 2][:, 0:CW], ACT.Relu, bias=b2).then_inc(r2_done, 1)

                def spread(l):
                    if tok:
                        condition(n, o + 1, [l])

                gate(0)
                if prs:
                    act.wait_ge(hT_psum, p + 1)
                    act.activation(hT[:, :], X[:, KD * S:KD * S + S], ACT.Copy).then_inc(hT_done, 1)
                if tok:
                    absolute(n, o + 1)
                    condition(n, o, [L - 1])
                top_copy(0)
                pair_relu(0, 1)
                pair_relu(1, 2)
                gate(1)
                relu(0)
                pair_relu(2, 3)
                relu(1)
                pair_relu(3, 4)
                top_copy(1)
                relu(2)
                relu(3)
                pair_relu(4, 6)
                gate(2)
                top_copy(2)
                relu(4)
                pair_relu(6, 8)
                if att:
                    act.wait_ge(exp_in, a + 1)
                    act.activation(prob[:, :, :], score[:, :, :], ACT.Exp, scale=HD ** -0.5).then_inc(exp_done, 1)
                gate(3)
                relu(5)
                relu(6)
                top_copy(3)
                spread(0)
                if tok:
                    act.wait_ge(tok_done, b + 1)
                    at_least(act, hx_done, b)
                    act.activation(h[:, :], C[0:S, 0:D], ACT.Identity, bias=tok_b).then_inc(h_done, 1)
                relu(7)
                if tok:
                    upsampled(n, o + 1, "top")
                    act.wait_ge(x_top, 5 * b + 5)
                    upsampled(n, o + 1, "bottom")
                if att:
                    act.wait_ge(aoT_psum, a + 1)
                    act.activation(aoT[0:KQ, :], G[0:KQ, 1, 0:S], ACT.Copy).then_inc(aoT_done, 1)
                if prs:
                    act.wait_ge(w3_done, 2 * p + 2)
                    at_least(act, sim_out, 16 * p)
                    act.activation(sim_rows[:, :], W[:, 0:CW], ACT.Identity, bias=b3).then_inc(sim_rows_done, 1)
                spread(1)
                spread(2)
                if tok:
                    act.wait_ge(xnT_psum, b + 1)
                    for k in range(KD):
                        ins = act.activation(xnT[:, k, :], X[:, S * k:S * k + S], ACT.Identity,
                                             bias=beta[:, k:k + 1], scale=gamma[:, k:k + 1])
                    ins.then_inc(xnT_done, 1)
            def first(n, o):
                absolute(n, o)
                condition(n, o, range(L - 1))
                for part in ("top", "bottom", "fifth"):
                    upsampled(n, o, part)
            schedule(act, step, first)

        @block.vector
        def _(dve):
            dve.memset(xs[:, :], 0.0)
            dve.memset(xc[0:CC, :, :, D - 2:], 0.0)
            dve.memset(off_diag[:, :], 1.0)
            dve.memset(aon[:, :], 0.0)
            dve.memset(enc[CC:CC + 1, :, :], 1.0)
            dve.memset(aoT[KQ:KQ + 1, :], 1.0).then_inc(h1_free, 16)
            dve.memset(minus_half[:, :], -0.5)
            dve.memset(ident[:, :], 0.0).then_inc(zeros_set, 1)
            dve.wait_ge(tok_w_in, 16 * 5)
            dve.wait_ge(const_chain, 2)
            dve.tensor_scalar(gate_b[:, :], gate_bias, 0.5, None, ALU.mult).then_inc(bn_ready, 1)
            dve.tensor_tensor(up_scale[:, :], bn_gamma, bn_rstd[:, :], ALU.mult).then_inc(bn_ready, 1)
            dve.tensor_tensor(up_shift[:, :], up_b, bn_mean, ALU.subtract).then_inc(const_chain, 1)
            dve.wait_ge(bn_ready, 2)
            dve.wait_ge(const_chain, 3)
            dve.scalar_tensor_tensor(up_shift[:, :], up_shift[:, :], up_scale[:, 0:1], bn_beta,
                                     ALU.mult, ALU.add).then_inc(bn_ready, 1)

            def recip(n, o, half):
                b = 2 * n + o
                q = slice(T * half, T * half + T)
                if half == 0:
                    dve.wait_ge(abs_done, b + 1)
                    dve.tensor_scalar(cabs[:, :], cabs[:, :], 1.0, None, ALU.add).then_inc(abs1_done, 1)
                    dve.wait_ge(abs1_done, b + 1)
                dve.reciprocal(cabs[:, q], cabs[:, q]).then_inc(recip_done, 1)

            def soften(n, o):
                b = 2 * n + o
                dve.wait_ge(recip_done, 2 * b + 2)
                at_least(dve, crep_done, L * b)
                dve.tensor_tensor(soft[:, :, :].rearrange("p q t -> p (q t)"), C[:, :], cabs[:, :],
                                  ALU.mult).then_inc(soft_done, 1)

            def step(n, o, tok, prs, att):
                b, p, a = 2 * n + o, 2 * n + o - 1, 2 * n + o - 2
                e = o % 2

                def conv_out(l):
                    if not tok:
                        return
                    dve.wait_ge(th_done, L * b + l + 1)
                    dve.scalar_tensor_tensor(gated[CC:, :], th[CC:, :], 1.0, Y[CC:, 0:D],
                                             ALU.add, ALU.mult).then_inc(gated_done, 1)
                    dve.wait_ge(gated_done, L * b + l + 1)
                    dve.scalar_tensor_tensor(xs[CC:, 1:1 + D], gated[CC:, :], 0.5, xs[CC:, 1:1 + D],
                                             ALU.mult, ALU.add).then_inc(x_bot, 1)

                def diff(lo, hi):
                    if not prs:
                        return
                    if lo == 0:
                        at_least(dve, z_done, NCH * p)
                    shape = [128, CH * (hi - lo), S]
                    dve.tensor_tensor(pair[:, lo:hi, :, :].rearrange("p c i j -> p (c i) j"),
                                      hT[:, CH * lo:CH * hi].unsqueeze(2).to_broadcast(shape),
                                      hT[:, :].unsqueeze(1).to_broadcast(shape),
                                      ALU.subtract).then_inc(diff_done, hi - lo)

                def stats_of(k, src):
                    dve.bn_stats(stats[:, k, :], src).then_inc(ln_chain, 1)

                def variance(k):
                    dve.bn_aggr(mv[:, k, :], stats[:, k, :]).then_inc(ln_chain, 1)
                    dve.wait_ge(ln_chain, 4 * b + 2 * k + 2)
                    dve.tensor_scalar(veps[:, k:k + 1], mv[:, k, 1:2], LN_EPS, None, ALU.add).then_inc(veps_done, 1)

                conv_out(0)
                if prs:
                    dve.wait_ge(hT_done, p + 1)
                diff(0, 1)
                diff(1, 2)
                diff(2, 3)
                if att:
                    dve.wait_ge(sim_done, a + 1)
                    dve.memset(turn[:, :], 0.0)
                    dve.max(top[:, :], sim[:, :]).then_inc(top_done, 1)
                    dve.wait_ge(top_done, a + 1)
                    dve.memset(turn[:, :], 0.0)
                    dve.max_index(idx[:, :], top[:, :], sim[:, :]).then_inc(idx_done, 1)
                diff(3, 4)
                if prs:
                    dve.wait_ge(qkv_psum, p + 1)
                    dve.tensor_tensor(qkv[:, (e + 1) % 2, :], G[0:S, 1, 0:3 * KQ], bqkv[:, :],
                                      ALU.add).then_inc(qkv_done, 1)
                conv_out(1)
                diff(4, 6)
                if tok:
                    recip(n, o + 1, 0)
                if att:
                    dve.wait_ge(idx_back, 16 * a + 16)
                    dve.tensor_scalar(pick[:, :, :], idx_all[:, :, :].rearrange("j i r -> j r i"), key_no[:, 0:1],
                                      None, ALU.is_equal).then_inc(pick_done, 1)
                diff(6, 8)
                conv_out(2)
                if tok:
                    recip(n, o + 1, 1)
                if att:
                    dve.wait_ge(g_done, a + 1)
                    gk = G[0:S, :, :].rearrange("i m (r c) -> i (m r) c", c=2 * KQ)
                    dve.tensor_tensor(prod[:, :, :], gk[:, :, 0:KQ],
                                      qkv[:, e, 0:KQ].unsqueeze(1).to_broadcast([S, TOPK, KQ]),
                                      ALU.mult).then_inc(at_chain, 1)
                    dve.wait_ge(at_chain, 7 * a + 1)
                    pr = prod[:, :, :].rearrange("i r (h d) -> i r h d", d=HD)
                    dve.tensor_tensor(score[:, :, :], pr[:, :, :, 0], pr[:, :, :, 1], ALU.add).then_inc(at_chain, 1)
                    dve.wait_ge(at_chain, 7 * a + 2)
                    dve.tensor_reduce(smax[:, :], score[:, :, :].rearrange("i r h -> i h r"), AX.X,
                                      ALU.max).then_inc(at_chain, 1)
                    dve.wait_ge(at_chain, 7 * a + 3)
                    dve.tensor_tensor(score[:, :, :], score[:, :, :],
                                      smax[:, :].unsqueeze(1).to_broadcast([S, TOPK, NH]),
                                      ALU.subtract).then_inc(exp_in, 1)
                if tok:
                    soften(n, o + 1)
                conv_out(3)
                if att:
                    dve.wait_ge(exp_done, a + 1)
                    dve.tensor_reduce(psum_[:, :], prob[:, :, :].rearrange("i r h -> i h r"), AX.X,
                                      ALU.add).then_inc(at_chain, 1)
                    for d in range(HD):
                        ins = dve.tensor_tensor(pv[:, :, :].rearrange("i r (h d) -> i r h d", d=HD)[:, :, :, d],
                                                gk[:, :, KQ:].rearrange("i r (h d) -> i r h d", d=HD)[:, :, :, d],
                                                prob[:, :, :], ALU.mult)
                    ins.then_inc(at_chain, 1)
                    dve.wait_ge(at_chain, 7 * a + 4)
                    dve.reciprocal(pinv[:, :], psum_[:, :]).then_inc(at_chain, 1)
                    dve.wait_ge(at_chain, 7 * a + 5)
                    dve.tensor_reduce(ao[:, :], pv[:, :, :].rearrange("i r c -> i c r"), AX.X,
                                      ALU.add).then_inc(at_chain, 1)
                    dve.wait_ge(at_chain, 7 * a + 7)
                    dve.tensor_tensor(aon[:, 0:KQ].rearrange("i (h d) -> i h d", d=HD),
                                      ao[:, :].rearrange("i (h d) -> i h d", d=HD),
                                      pinv[:, :].unsqueeze(2).to_broadcast([S, NH, HD]), ALU.mult).then_inc(ao_done, 1)
                if tok:
                    dve.wait_ge(h_done, b + 1)
                    stats_of(0, h[:, :])
                if tok:
                    dve.wait_ge(ln_chain, 4 * b + 1)
                    dve.memset(turn[:, :], 0.0)
                    variance(0)
                    dve.wait_ge(x_top, 5 * b + 6)
                    dve.tensor_copy(xc[0:CC, 1 - e, 0, 0:D - 2], xs[0:CC, 4:2 + D]).then_inc(xc_top, 1)
                    dve.wait_ge(rstd_done, 2 * b + 1)
                    at_least(dve, hx_done, b)
                    dve.tensor_scalar(xa[:, :], h[:, :], mv[:, 0, 0:1], rstd[:, 0:1], ALU.subtract,
                                      ALU.mult).then_inc(xa_done, 1)
                    dve.wait_ge(xa_done, b + 1)
                    stats_of(1, xa[:, :])
                    dve.wait_ge(ln_chain, 4 * b + 3)
                    dve.memset(turn[:, :], 0.0)
                    variance(1)
                    dve.wait_ge(rstd_done, 2 * b + 2)
                    at_least(dve, xnT_psum, b)
                    dve.tensor_scalar(xn[:, :], xa[:, :], mv[:, 1, 0:1], rstd[:, 1:2], ALU.subtract,
                                      ALU.mult).then_inc(xn_done, 1)
                if att:
                    dve.wait_ge(wo_done, a + 1)
                    dve.wait_ge(hx_done, a + 1)
                    dve.wait_ge(h1_free, 16 * a + 16)
                    dve.tensor_tensor(h1[:, :], G[0:S, 0, 0:D], hx[:, e, :], ALU.add).then_inc(h1_done, 1)
            def first(n, o):
                recip(n, o, 0)
                recip(n, o, 1)
                soften(n, o)
                dve.wait_ge(att_w_in, 16 * 6)

            schedule(dve, step, first)


def experts(nc, t, eg_w, ed_w, region):
    N, D = t["h1f"].shape
    KD = D // 128
    E = t["gateT"].shape[1] - 1
    FS = t["sharedT"].shape[1] // (3 * KD)
    SF = FS // 128
    I = t["edT"].shape[1]
    IH = I // 2
    TOP = 2
    J = N // 128
    BLOCKS = (TOP * N - E) // 128 + E
    BLOCKS += BLOCKS % 2

    xn_d = nc.dram_tensor("xn_d", (N, D), F32, kind="Internal").ap()
    y_d = nc.dram_tensor("y_d", (BLOCKS * 128, D), F32, kind="Internal").ap()

    def maker(ctx):
        def sb(name, shape, dt=F32):
            return ctx.enter_context(nc.sbuf_tensor("ffn_" + name, shape, dt))

        def ps(name, shape):
            return ctx.enter_context(nc.psum_tensor("ffn_" + name, shape, F32))

        def sem(name):
            return ctx.enter_context(nc.semaphore("ffn_" + name))
        return sb, ps, sem

    def rows(ap, first, count):
        return ap[first:first + count] if isinstance(first, int) else ap[bass.ds(first, count)]

    whole = ExitStack()
    sb, _, _ = maker(whole)
    SHARED = 2 * KD * FS + SF * D
    w_hi, w_lo = sb("w_hi", [128, SHARED], F32R), sb("w_lo", [128, SHARED], F32R)

    def shared_weight(w, which):
        at = KD * FS * which
        if which < 2:
            return w[:, at:at + KD * FS].rearrange("p (k f) -> p k f", k=KD)
        return w[:, at:].rearrange("p (k d) -> p k d", k=SF)
    sg_hi, su_hi, sd_hi = [shared_weight(w_hi, k) for k in range(3)]
    sg_lo, su_lo, sd_lo = [shared_weight(w_lo, k) for k in range(3)]
    ident = sb("ident", [128, 128])
    slot_u = sb("slot_u", [128, TOP, J], U32)
    weight = sb("weight", [128, TOP, J])
    shared_gate = sb("shared_gate", [128, J])


    def norm_and_logits(ctx, LG):
        sb, ps, sem = maker(ctx)
        U = 4
        rt_w = sb("rt_w", [128, KD, E + 1])
        minus_half = sb("minus_half", [128, 1])
        turn = sb("turn", [1, 1])
        h_in = sb("h_in", [128, U, D])
        xn = sb("xn", [128, U, D])
        xT = sb("xT", [128, 2, KD, 128])
        stats = sb("stats", [128, 2, 6])
        mv = sb("mv", [128, 2, 2])
        veps = sb("veps", [128, 2])
        rstd = sb("rstd", [128, 2])
        XP = [ps("XP0", [128, D]), ps("XP1", [128, D])]
        router_in, zeros, ident_done = sem("router_in"), sem("zeros"), sem("ident_done")
        h_loaded = [sem(f"h_loaded{k}") for k in range(U)]
        xn_out = [sem(f"xn_out{k}") for k in range(U)]
        stats_done, aggr_done, veps_done, rstd_done = [sem(k) for k in ("stats_done", "aggr_done", "veps_done", "rstd_done")]
        xn_done, xT_psum, xT_done, lg_done = [sem(k) for k in ("xn_done", "xT_psum", "xT_done", "lg_done")]

        def schedule(eng, step):
            for n in range(2):
                for o in range(U):
                    step(n, o, True, n + o > 0)
            with eng.Fori(2, J // U - 1) as n:
                for o in range(U):
                    step(n, o, True, True)
            for o in range(U):
                step(J // U - 1, o, True, True)
            step(J // U, 0, False, True)

        with nc.Block() as block:
            @block.sync
            def _(sp):
                def load(n, o):
                    j = U * n + o
                    if isinstance(j, int) and j >= J:
                        return
                    at_least(sp, xn_done, j - U + 1)
                    sp.dma_start(h_in[:, o % U, :], rows(t["h1f"], 128 * j, 128)).then_inc(h_loaded[o % U], 16)

                sp.dma_start(rt_w[:, :, :], t["gateT"].rearrange("(k p) f -> p k f", p=128)).then_inc(router_in, 16)
                load(0, 0)
                load(0, 1)

                def step(n, o, start, finish):
                    j = U * n + o
                    if start:
                        load(n, o + 2)
                    if finish:
                        sp.wait_ge(xn_done, j)
                        sp.dma_start(rows(xn_d, 128 * (j - 1), 128), xn[:, (o - 1) % U, :]).then_inc(xn_out[(o - 1) % U], 16)
                schedule(sp, step)
                for k in range(U):
                    sp.wait_ge(xn_out[k], 16 * (J // U))

            @block.gpsimd
            def _(pool):
                pool.wait_ge(zeros, 1)
                pool.affine_select(out=ident[:, :], in_=ident[:, :], compare_op=ALU.not_equal, fill=1.0,
                                   base=0, pattern=[[-1, 128]], channel_multiplier=1).then_inc(ident_done, 1)

                def step(n, o, start, finish):
                    if start:
                        q = slice(o % 2, o % 2 + 1)
                        pool.wait_ge(veps_done, U * n + o + 1)
                        pool.tensor_tensor(rstd[:, q], veps[:, q], minus_half[:, :], ALU.pow).then_inc(rstd_done, 1)
                schedule(pool, step)

            @block.tensor
            def _(pe):
                pe.wait_ge(ident_done, 1)
                pe.wait_ge(router_in, 16)

                def step(n, o, start, finish):
                    j = U * n + o
                    if finish:
                        pe.wait_ge(xn_done, j)
                        for k in range(KD):
                            mm = pe.transpose(XP[(o + 1) % 2][:, 128 * k:128 * k + 128],
                                              xn[:, (o - 1) % U, 128 * k:128 * k + 128], ident[:, :])
                        mm.then_inc(xT_psum, 1)
                    if not (isinstance(j, int) and j < 2):
                        logits(j - 2, o)

                def logits(j, o):
                    pe.wait_ge(xT_done, j + 1)
                    at = LG[:, j, :] if isinstance(j, int) else LG[:, bass.ds(j, 1), :].squeeze(1)
                    for k in range(KD):
                        mm = pe.matmul(at, xT[:, o % 2, k, :], rt_w[:, k, :], start=(k == 0), stop=(k == KD - 1))
                    mm.then_inc(lg_done, 1)
                schedule(pe, step)
                logits(J - 1, 1)

            @block.scalar
            def _(act):
                def step(n, o, start, finish):
                    j = U * n + o
                    if finish:
                        act.wait_ge(xT_psum, j)
                        at_least(act, lg_done, j - 2)
                        act.activation(xT[:, (o + 1) % 2, :, :].rearrange("p k c -> p (k c)"), XP[(o + 1) % 2][:, :],
                                       ACT.Copy).then_inc(xT_done, 1)
                schedule(act, step)

            @block.vector
            def _(dve):
                dve.memset(minus_half[:, :], -0.5)
                dve.memset(ident[:, :], 0.0).then_inc(zeros, 1)

                def step(n, o, start, finish):
                    j = U * n + o
                    q, r = o % 2, (o + 1) % 2
                    if start:
                        dve.wait_ge(h_loaded[o], 16 * n + 16)
                        dve.bn_stats(stats[:, q, :], h_in[:, o, :]).then_inc(stats_done, 1)
                        dve.wait_ge(stats_done, j + 1)
                    if finish:
                        dve.wait_ge(rstd_done, j)
                        at_least(dve, xT_psum, j - U)
                        if not isinstance(j, int) or j > U:
                            dve.wait_ge(xn_out[(o - 1) % U], 16 * (n if o else n - 1))
                        dve.tensor_scalar(xn[:, (o - 1) % U, :], h_in[:, (o - 1) % U, :], mv[:, r, 0:1], rstd[:, r:r + 1],
                                          ALU.subtract, ALU.mult).then_inc(xn_done, 1)
                    else:
                        dve.memset(turn[:, :], 0.0)
                    if start:
                        dve.bn_aggr(mv[:, q, :], stats[:, q, :]).then_inc(aggr_done, 1)
                        dve.wait_ge(aggr_done, j + 1)
                        dve.tensor_scalar(veps[:, q:q + 1], mv[:, q, 1:2], LN_EPS, None, ALU.add).then_inc(veps_done, 1)
                schedule(dve, step)

    def slots(ctx, slot_token, block_expert, LG):
        sb, ps, sem = maker(ctx)
        CHK = 4
        BIG = 12582912.0
        e_no = sb("e_no", [128, E])
        tile_no = sb("tile_no", [128, J])
        token_no = sb("token_no", [128, J])
        col_no = sb("col_no", [128, 128])
        before = sb("before", [128, 128])
        ones = sb("ones", [128, 128])
        turn = sb("turn2", [1, 1])
        lg = sb("lg", [128, J, E + 1])
        lmax = sb("lmax", [128, J])
        probs = sb("probs", [128, J, E])
        total = sb("total", [128, J])
        top = sb("top", [128, J, 8])
        idx = sb("idx", [128, J, 8], U32)
        chosen = sb("chosen", [128, TOP, J, E])
        both = sb("both", [128, J, E])
        run = [sb("run0", [128, J, E]), sb("run1", [128, J, E])]
        place = sb("place", [128, J, E])
        filled = sb("filled", [128, E, J])
        blocks = sb("blocks", [128, 3, E])
        start = sb("start", [128, E])
        slot = sb("slot", [128, TOP, J])
        slot_block = sb("slot_block", [128, TOP, J])
        slot_row = sb("slot_row", [128, TOP, J])
        hot_row = sb("hot_row", [128, 2, CHK, 128])
        hot_block = sb("hot_block", [128, 2, CHK, BLOCKS])
        block_no = sb("block_no", [1, BLOCKS, E - 1])
        ended = sb("ended", [1, BLOCKS, E - 1])
        expert_f = sb("expert_f", [1, BLOCKS])
        RANK, TILE = ps("RANK", [128, J, E]), ps("TILE", [128, J, E])
        TABLE = ps("TABLE", [128, BLOCKS])
        set_, consts, lg_out, exp_in, exp_out, gate_out = [sem(k) for k in ("set", "consts", "lg_out", "exp_in", "exp_out", "gate_out")]
        chain, both_done, ranks_done, hot_done, table_used = [sem(k) for k in ("chain", "both_done", "ranks_done", "hot_done", "table_used")]
        flat = "p j e -> p (j e)"

        with nc.Block() as block:
            @block.gpsimd
            def _(pool):
                exact = dict(allow_small_or_imprecise_dtypes=True)
                pool.iota(e_no[:, :], [[1, E]], base=0, channel_multiplier=0, **exact).then_inc(consts, 1)
                pool.iota(tile_no[:, :], [[128, J]], base=0, channel_multiplier=0, **exact).then_inc(consts, 1)
                pool.iota(token_no[:, :], [[128, J]], base=0, channel_multiplier=1, **exact).then_inc(consts, 1)
                pool.iota(col_no[:, :], [[1, 128]], base=0, channel_multiplier=0, **exact).then_inc(consts, 1)
                pool.iota(block_no[:, :, :], [[1, BLOCKS], [0, E - 1]], base=0, channel_multiplier=0,
                          **exact).then_inc(consts, 1)
                pool.wait_ge(set_, 1)
                pool.affine_select(out=before[:, :], in_=ones[:, :], compare_op=ALU.is_gt, fill=0.0,
                                   base=0, pattern=[[1, 128]], channel_multiplier=-1).then_inc(consts, 1)

            @block.scalar
            def _(act):
                act.activation(lg[:, :, :], LG[:, :, :], ACT.Copy).then_inc(lg_out, 1)
                act.wait_ge(exp_in, 1)
                act.activation(probs[:, :, :], probs[:, :, :], ACT.Exp).then_inc(exp_out, 1)
                act.activation(shared_gate[:, :], lg[:, :, E], ACT.Tanh, scale=0.5).then_inc(gate_out, 1)

            @block.tensor
            def _(pe):
                pe.wait_ge(consts, 6)
                pe.wait_ge(both_done, 1)
                pe.matmul(RANK[:, :, :].rearrange(flat), before[:, :], both[:, :, :].rearrange(flat),
                          start=True, stop=True)
                pe.matmul(TILE[:, :, :].rearrange(flat), ones[:, :], both[:, :, :].rearrange(flat),
                          start=True, stop=True).then_inc(ranks_done, 1)
                last = TOP * J // CHK - 1
                for c in range(last + 1):
                    pe.wait_ge(hot_done, 2 * c + 2)
                    for i in range(CHK):
                        mm = pe.matmul(TABLE[:, :], hot_row[:, c % 2, i, :], hot_block[:, c % 2, i, :],
                                       start=(c == 0 and i == 0), stop=(c == last and i == CHK - 1))
                    mm.then_inc(table_used, 1)

            @block.vector
            def _(dve):
                count = [0]

                def then(ins):
                    count[0] += 1
                    ins.then_inc(chain, 1)
                    dve.wait_ge(chain, count[0])

                def wide(ap):
                    return ap.unsqueeze(2).to_broadcast([128, J, E])

                dve.memset(ones[:, :], 1.0).then_inc(set_, 1)
                dve.wait_ge(lg_out, 1)
                then(dve.tensor_reduce(lmax[:, :], lg[:, :, 0:E], AX.X, ALU.max))
                dve.tensor_tensor(probs[:, :, :], lg[:, :, 0:E], wide(lmax[:, :]), ALU.subtract).then_inc(exp_in, 1)
                dve.wait_ge(exp_out, 1)
                then(dve.tensor_reduce(total[:, :], probs[:, :, :], AX.X, ALU.add))
                then(dve.reciprocal(total[:, :], total[:, :]))
                then(dve.tensor_tensor(probs[:, :, :], probs[:, :, :], wide(total[:, :]), ALU.mult))
                for j in range(J):
                    ins = dve.max(top[:, j, :], probs[:, j, :])
                then(ins)
                for j in range(J):
                    ins = dve.max_index(idx[:, j, :], top[:, j, :], probs[:, j, :])
                then(ins)
                dve.wait_ge(consts, 6)
                for k in range(TOP):
                    ins = dve.tensor_tensor(chosen[:, k, :, :], e_no[:, :].unsqueeze(1).to_broadcast([128, J, E]),
                                            idx[:, :, k:k + 1].to_broadcast([128, J, E]), ALU.is_equal)
                then(ins)
                dve.tensor_tensor(both[:, :, :], chosen[:, 0, :, :], chosen[:, 1, :, :], ALU.add).then_inc(both_done, 1)
                then(dve.tensor_tensor(total[:, :], top[:, :, 0], top[:, :, 1], ALU.add))
                then(dve.reciprocal(total[:, :], total[:, :]))
                for k in range(TOP):
                    dve.scalar_tensor_tensor(weight[:, k, :], total[:, :], 0.5, top[:, :, k], ALU.mult, ALU.mult)
                dve.wait_ge(gate_out, 1)
                dve.tensor_scalar(shared_gate[:, :], shared_gate[:, :], 0.25, 0.25, ALU.mult, ALU.add)
                dve.wait_ge(ranks_done, 1)
                then(dve.tensor_copy(run[0][:, :, :], TILE[:, :, :]))
                step, now = 1, 0
                while step < J:
                    a, b = run[now], run[1 - now]
                    dve.tensor_copy(b[:, 0:step, :], a[:, 0:step, :])
                    then(dve.tensor_tensor(b[:, step:, :], a[:, step:, :], a[:, 0:J - step, :], ALU.add))
                    step, now = 2 * step, 1 - now
                upto = run[now]
                then(dve.tensor_tensor(filled[:, :, :], upto[:, J - 1, :].unsqueeze(2).to_broadcast([128, E, J]),
                                       tile_no[:, :].unsqueeze(1).to_broadcast([128, E, J]), ALU.is_gt))
                then(dve.tensor_reduce(blocks[:, 0, :], filled[:, :, :], AX.X, ALU.add))
                then(dve.tensor_copy(blocks[:, 1, :], blocks[:, 0, :]))
                step, now = 1, 1
                while step < E:
                    a, b = blocks[:, now, :], blocks[:, 3 - now, :]
                    dve.tensor_copy(b[:, 0:step], a[:, 0:step])
                    then(dve.tensor_tensor(b[:, step:], a[:, step:], a[:, 0:E - step], ALU.add))
                    step, now = 2 * step, 3 - now
                ends = blocks[:, now, :]
                then(dve.tensor_tensor(start[:, :], ends, blocks[:, 0, :], ALU.subtract))
                then(dve.tensor_scalar(start[:, :], start[:, :], 128.0, None, ALU.mult))
                then(dve.tensor_tensor(place[:, :, :], RANK[:, :, :], upto[:, :, :], ALU.add))
                then(dve.tensor_tensor(place[:, :, :], place[:, :, :], TILE[:, :, :], ALU.subtract))
                then(dve.tensor_tensor(place[:, :, :], place[:, :, :],
                                       start[:, :].unsqueeze(1).to_broadcast([128, J, E]), ALU.add))
                for k in range(TOP):
                    ins = dve.tensor_tensor(chosen[:, k, :, :], chosen[:, k, :, :], place[:, :, :], ALU.mult)
                then(ins)
                then(dve.tensor_reduce(slot[:, :, :], chosen[:, :, :, :], AX.X, ALU.add))
                dve.tensor_copy(slot_u[:, :, :], slot[:, :, :])
                then(dve.tensor_scalar(slot_block[:, :, :], slot[:, :, :], 1.0 / 128, -63.5 / 128, ALU.mult, ALU.add))
                then(dve.tensor_scalar(slot_block[:, :, :], slot_block[:, :, :], BIG, None, ALU.add))
                then(dve.tensor_scalar(slot_block[:, :, :], slot_block[:, :, :], -BIG, None, ALU.add))
                then(dve.scalar_tensor_tensor(slot_row[:, :, :], slot_block[:, :, :], -128.0, slot[:, :, :],
                                              ALU.mult, ALU.add))
                then(dve.tensor_tensor(ended[:, :, :], block_no[:, :, :],
                                       ends[0:1, 0:E - 1].unsqueeze(1).to_broadcast([1, BLOCKS, E - 1]), ALU.is_ge))
                then(dve.tensor_reduce(expert_f[:, :], ended[:, :, :], AX.X, ALU.add))
                then(dve.tensor_copy(block_expert[:, :], expert_f[:, :]))
                for c in range(TOP * J // CHK):
                    k, js, q = c // (J // CHK), slice(c % (J // CHK) * CHK, c % (J // CHK) * CHK + CHK), c % 2
                    if c >= 2:
                        dve.wait_ge(table_used, c - 1)
                    dve.tensor_tensor(hot_row[:, q, :, :], col_no[:, :].unsqueeze(1).to_broadcast([128, CHK, 128]),
                                      slot_row[:, k, js].unsqueeze(2).to_broadcast([128, CHK, 128]),
                                      ALU.is_equal).then_inc(hot_done, 1)
                    then(dve.tensor_tensor(hot_block[:, q, :, :],
                                           col_no[:, 0:BLOCKS].unsqueeze(1).to_broadcast([128, CHK, BLOCKS]),
                                           slot_block[:, k, js].unsqueeze(2).to_broadcast([128, CHK, BLOCKS]),
                                           ALU.is_equal))
                    dve.tensor_tensor(hot_block[:, q, :, :], hot_block[:, q, :, :],
                                      token_no[:, js].unsqueeze(2).to_broadcast([128, CHK, BLOCKS]),
                                      ALU.mult).then_inc(hot_done, 1)
                dve.wait_ge(table_used, TOP * J // CHK)
                then(dve.tensor_copy(slot_token[:, :], TABLE[:, :]))

    def routed_experts(ctx, slot_token, block_expert):
        sb, ps, sem = maker(ctx)
        x = sb("x", [128, 2, D])
        carry = sb("r_carry", [1, 1])
        token = sb("token", [128, 2], U32)
        xT = sb("x_T", [128, 2, KD, 128])
        th = sb("th", [128, I])
        hidden = sb("hidden", [128, 2, I])
        hT = sb("h_T", [IH, 2, 128])
        y = sb("y", [128, 2, D])
        XP = [ps("RXP0", [128, D]), ps("RXP1", [128, D])]
        GU = [ps("RGU0", [128, 512]), ps("RGU1", [128, 512])]
        HP = ps("RHP", [IH, 2, 128])
        Y = [ps("RY0", [128, D]), ps("RY1", [128, D])]
        x_in = [sem("x_in0"), sem("x_in1")]
        y_out = [sem("y_out0"), sem("y_out1")]
        token_set = sem("token_set")
        x_psum, xT_done, gu_done, th_done = [sem("r_" + k) for k in ("x_psum", "xT_done", "gu_done", "th_done")]
        gated_done, hidden_done, h_psum, hT_done, down_done, y_done = [
            sem("r_" + k) for k in ("gated_done", "hidden_done", "h_psum", "hT_done", "down_done", "y_done")]

        PIECE = 512
        PIECES = SHARED // PIECE
        raw = sb("raw", [128, 2, PIECE])
        raw_in = [sem("raw_in0"), sem("raw_in1")]
        rounded, rest_done = sem("rounded"), sem("rest_done")

        def schedule(eng, step, split=None, load=None):
            PAIRS = BLOCKS // 2
            assert PIECES + 2 < PAIRS - 1 and PIECES % 2 == 0
            for n in range(2):
                step(n, 0, True, n > 0)
                step(n, 1, True, True)
            def pair_with_piece(m, o):
                if load:
                    load(m, o)
                step(2 * m + o + 2, 0, True, True)
                step(2 * m + o + 2, 1, True, True)
                if split:
                    split(m, o)
            pair_with_piece(0, 0)
            pair_with_piece(0, 1)
            with eng.Fori(1, PIECES // 2) as m:
                pair_with_piece(m, 0)
                pair_with_piece(m, 1)
            with eng.Fori(PIECES + 2, PAIRS - 1) as n:
                step(n, 0, True, True)
                step(n, 1, True, True)
            step(PAIRS - 1, 0, True, True)
            step(PAIRS - 1, 1, True, True)
            step(PAIRS, 0, False, True)

        def piece(ap, m, o):
            at = PIECE * (2 * m + o)
            return ap[:, at:at + PIECE] if isinstance(m, int) else ap[:, bass.ds(at, PIECE)]

        def at(ap, i):
            return ap[:, i:i + 1] if isinstance(i, int) else ap[:, bass.ds(i, 1)]

        with nc.Block() as block:
            @block.gpsimd
            def _(pool):
                def gather(n, o):
                    i, q = 2 * n + o, o % 2
                    pool.tensor_copy(token[:, q:q + 1], at(slot_token, i)).then_inc(token_set, 1)
                    pool.wait_ge(token_set, i + 1)
                    pool.tensor_tensor(carry[:, :], ident[0:1, 0:1], ident[0:1, 0:1], ALU.mult)
                    pool.indirect_dma_start(x[:, q, :], None, xn_d, bass.IndirectOffsetOnAxis(token[:, q:q + 1], 0)
                                            ).then_inc(x_in[q], 16)
                gather(0, 0)
                gather(0, 1)

                def step(n, o, start, finish):
                    i = 2 * n + o
                    if start and not (isinstance(i, int) and i + 2 >= BLOCKS):
                        pool.wait_ge(x_psum, i + 1)
                        gather(n, o + 2)
                schedule(pool, step)

            @block.tensor
            def _(pe):
                def expert(i):
                    return pe.value_load(at(block_expert, i), min_val=0, max_val=E - 1)

                def turn(n, o):
                    i, q = 2 * n + o, o % 2
                    pe.wait_ge(x_in[q], 16 * (n + o // 2) + 16)
                    for k in range(KD):
                        mm = pe.transpose(XP[q][:, 128 * k:128 * k + 128], x[:, q, 128 * k:128 * k + 128], ident[:, :])
                    mm.then_inc(x_psum, 1)

                def turn_hidden(i, q):
                    pe.wait_ge(hidden_done, i + 1)
                    for m in range(2):
                        mm = pe.transpose(HP[:, m, :], hidden[:, q, IH * m:IH * m + IH], ident[:, :])
                    mm.then_inc(h_psum, 1)

                turn(0, 0)

                def step(n, o, start, finish):
                    i, q, r = 2 * n + o, o % 2, (o + 1) % 2
                    if start:
                        e = expert(i)
                        pe.wait_ge(xT_done, i + 1)
                        for k in range(KD):
                            mm = pe.matmul(GU[q][:, 0:2 * I], xT[:, q, k, :], eg_w[:, k, bass.ds(e, 1), :].squeeze(1),
                                           start=(k == 0), stop=(k == KD - 1))
                            if k == KD // 2 and finish:
                                turn_hidden(i - 1, r)
                        mm.then_inc(gu_done, 1)
                    elif finish:
                        turn_hidden(i - 1, r)
                    if start and not (isinstance(i, int) and i + 1 >= BLOCKS):
                        turn(n, o + 1)
                    if finish:
                        e = expert(i - 1)
                        pe.wait_ge(hT_done, i)
                        at_least(pe, y_done, i - 2)
                        for m in range(2):
                            mm = pe.matmul(Y[r][:, :], hT[:, m, :], ed_w[:, bass.ds(e, 1), m, :].squeeze(1),
                                           start=(m == 0), stop=(m == 1))
                        mm.then_inc(down_done, 1)
                schedule(pe, step)

            @block.scalar
            def _(act):
                def turned(n, o):
                    i, q = 2 * n + o, o % 2
                    act.wait_ge(x_psum, i + 1)
                    act.activation(xT[:, q, :, :].rearrange("p k c -> p (k c)"), XP[q][:, :], ACT.Copy).then_inc(xT_done, 1)
                turned(0, 0)

                def step(n, o, start, finish):
                    i, q = 2 * n + o, o % 2
                    if finish:
                        act.wait_ge(h_psum, i)
                        at_least(act, down_done, i - 1)
                        act.activation(hT[:, :, :], HP[:, :, :], ACT.Copy).then_inc(hT_done, 1)
                    if start:
                        act.wait_ge(gu_done, i + 1)
                        at_least(act, gated_done, i)
                        act.activation(th[:, :], GU[q][:, 0:I], ACT.Tanh, scale=0.5).then_inc(th_done, 1)
                    if start and not (isinstance(i, int) and i + 1 >= BLOCKS):
                        turned(n, o + 1)

                def split(m, o):
                    act.wait_ge(raw_in[o], 16 * m + 16)
                    act.activation(piece(w_hi, m, o), raw[:, o, :], ACT.Copy).then_inc(rounded, 1)
                schedule(act, step, split)

            @block.vector
            def _(dve):
                def step(n, o, start, finish):
                    i, q, r = 2 * n + o, o % 2, (o + 1) % 2
                    if start:
                        dve.wait_ge(th_done, i + 1)
                        at_least(dve, h_psum, i - 1)
                        dve.scalar_tensor_tensor(hidden[:, q, :], th[:, :], 1.0, GU[q][:, 0:I], ALU.add,
                                                 ALU.mult).then_inc(gated_done, 1)
                        dve.wait_ge(gated_done, i + 1)
                        dve.tensor_tensor(hidden[:, q, :], hidden[:, q, :], GU[q][:, I:2 * I],
                                          ALU.mult).then_inc(hidden_done, 1)
                    if finish:
                        dve.wait_ge(down_done, i)
                        if not isinstance(i, int) or i >= 3:
                            dve.wait_ge(y_out[r], 16 * (n if o else n - 1))
                        dve.tensor_copy(y[:, r, :], Y[r][:, :]).then_inc(y_done, 1)

                def split(m, o):
                    dve.wait_ge(rounded, 2 * m + o + 1)
                    dve.tensor_tensor(piece(w_lo, m, o), raw[:, o, :], piece(w_hi, m, o).bitcast(F32),
                                      ALU.subtract).then_inc(rest_done, 1)
                schedule(dve, step, split)

            @block.sync
            def _(sp):
                def step(n, o, start, finish):
                    i, r = 2 * n + o, (o + 1) % 2
                    if finish:
                        sp.wait_ge(y_done, i)
                        sp.dma_start(rows(y_d, 128 * (i - 1), 128), y[:, r, :]).then_inc(y_out[r], 16)

                def load(m, o):
                    at_least(sp, rest_done, 2 * m + o - 1)
                    sp.dma_start(raw[:, o, :], piece(t["sharedT"], m, o)).then_inc(raw_in[o], 16)
                schedule(sp, step, load=load)
                for q in range(2):
                    sp.wait_ge(y_out[q], 16 * (BLOCKS // 2))

    def shared_expert(ctx):
        sb, ps, sem = maker(ctx)
        NT = 512
        TT = NT // 128
        TILES = N // NT
        ROWS = TT * D
        xn = region[:, 0:ROWS].rearrange("p (a d) -> p a d", a=TT)
        h = region[:, ROWS:3 * ROWS].rearrange("p (q a d) -> p q a d", q=2, a=TT)
        y_rows = region[:, 3 * ROWS:(3 + TOP) * ROWS].rearrange("p (k a d) -> p k a d", k=TOP, a=TT)
        free = (3 + TOP) * ROWS
        th, hidden = region[:, free:free + NT], region[:, free + NT:free + 2 * NT]
        x_hi, x_lo = sb("x_hi", [128, KD, NT], F32R), sb("x_lo", [128, KD, NT], F32R)
        hid_hi, hid_lo = sb("hid_hi", [128, 2, NT], F32R), sb("hid_lo", [128, 2, NT], F32R)
        carry = sb("s_carry", [1, TT])
        row = sb("row", [128, TOP, TT], U32)
        GU = [ps(f"GU{k}", [128, NT]) for k in range(4)]
        OUT = [ps(f"OUT{k}", [128, D]) for k in range(TT)]
        h_in, xn_in, y_in, out_out = [sem("h_in0"), sem("h_in1")], sem("s_xn_in"), sem("y_in"), [sem("out_out0"), sem("out_out1")]
        x_psum, hi_done, x_done, gu_done, th_done = [sem("s_" + k) for k in ("x_psum", "hi_done", "x_done", "gu_done", "th_done")]
        gated_done, hidden_done, hid_hi_done, hid_done, down_done = [
            sem("s_" + k) for k in ("gated_done", "hidden_done", "hid_hi_done", "hid_done", "down_done")]
        row_set = sem("row_set")
        sum_done, first_done, out_done = sem("s_sum_done"), sem("s_first_done"), sem("s_out_done")

        def schedule(eng, step):
            step(0, 0)
            step(0, 1)
            with eng.Fori(1, TILES // 2 - 1) as n:
                step(n, 0)
                step(n, 1)
            step(TILES // 2 - 1, 0)
            step(TILES // 2 - 1, 1)

        def last(i):
            return isinstance(i, int) and i >= TILES

        with nc.Block() as block:
            @block.sync
            def _(sp):
                def load(n, o):
                    i = 2 * n + o
                    if last(i):
                        return
                    at_least(sp, x_psum, KD * i)
                    sp.dma_start(xn[:, :, :], rows(xn_d, NT * i, NT).rearrange("(a p) d -> p a d", p=128)).then_inc(xn_in, 16)
                    if not isinstance(i, int) or i >= 2:
                        sp.wait_ge(out_out[o % 2], 16 * (n + o // 2))
                    sp.dma_start(h[:, o % 2, :, :], rows(t["h1f"], NT * i, NT).rearrange("(a p) d -> p a d", p=128)
                                 ).then_inc(h_in[o % 2], 16)
                load(0, 0)

                def step(n, o):
                    i = 2 * n + o
                    load(n, o + 1)
                    sp.wait_ge(out_done, TT * i + TT)
                    sp.dma_start(rows(t["out"], NT * i, NT).rearrange("(a p) d -> p a d", p=128),
                                 h[:, o % 2, :, :]).then_inc(out_out[o % 2], 16)
                schedule(sp, step)
                for q in range(2):
                    sp.wait_ge(out_out[q], 16 * (TILES // 2))

            @block.gpsimd
            def _(pool):
                def step(n, o):
                    i = 2 * n + o
                    at_least(pool, y_in, 16 * TOP * TT * i)
                    pool.tensor_copy(row[:, :, :], slot_u[:, :, bass.ds(TT * i, TT)]).then_inc(row_set, 1)
                    pool.wait_ge(row_set, i + 1)
                    for a in range(TT):
                        if not (isinstance(i, int) and i == 0):
                            pool.wait_ge(out_done, TT * (i - 1) + a + 1)
                        pool.tensor_tensor(carry[:, a:a + 1], ident[0:1, 0:1], ident[0:1, 0:1], ALU.mult)
                        for k in range(TOP):
                            pool.indirect_dma_start(y_rows[:, k, a, :], None, y_d,
                                                    bass.IndirectOffsetOnAxis(row[:, k, a:a + 1], 0)).then_inc(y_in, 16)
                schedule(pool, step)

            @block.tensor
            def _(pe):
                def turn(i, ks):
                    for k in ks:
                        for a in range(TT):
                            mm = pe.transpose(GU[k][:, 128 * a:128 * a + 128], xn[:, a, 128 * k:128 * k + 128], ident[:, :])
                        mm.then_inc(x_psum, 1)

                pe.wait_ge(xn_in, 16)
                turn(0, range(KD))

                def parts(out, a_hi, a_lo, b_hi, b_lo, first, final):
                    pe.matmul(out, a_hi, b_hi, start=first, stop=False)
                    pe.matmul(out, a_hi, b_lo, start=False, stop=False)
                    return pe.matmul(out, a_lo, b_hi, start=False, stop=final)

                def step(n, o):
                    i = 2 * n + o

                    def down(j):
                        pe.wait_ge(hid_done, SF * i + j + 1)
                        if j == 0:
                            at_least(pe, sum_done, TT * i)
                        q = j % 2
                        for a in range(TT):
                            c = slice(128 * a, 128 * a + 128)
                            mm = parts(OUT[a][:, :], hid_hi[:, q, c], hid_lo[:, q, c], sd_hi[:, j, :], sd_lo[:, j, :],
                                       j == 0, j == SF - 1)
                        mm.then_inc(down_done, 1)

                    pe.wait_ge(x_done, KD * i + KD)
                    for j in range(SF):
                        f, q = slice(128 * j, 128 * j + 128), j % 2
                        if j >= 2:
                            pe.wait_ge(hidden_done, SF * i + j - 1)
                        for bank, hi, lo in ((GU[2 * q], sg_hi, sg_lo), (GU[2 * q + 1], su_hi, su_lo)):
                            for k in range(KD):
                                mm = parts(bank[:, :], hi[:, k, f], lo[:, k, f], x_hi[:, k, :], x_lo[:, k, :],
                                           k == 0, k == KD - 1)
                            mm.then_inc(gu_done, 1)
                        if j:
                            down(j - 1)
                    more = not last(i + 1)
                    if more:
                        pe.wait_ge(xn_in, 16 * (i + 2))
                        turn(i + 1, range(0, 2))
                        pe.wait_ge(hidden_done, SF * i + SF)
                        turn(i + 1, range(2, KD))
                    down(SF - 1)
                schedule(pe, step)

            @block.scalar
            def _(act):
                def rounded(i):
                    for k in range(KD):
                        act.wait_ge(x_psum, KD * i + k + 1)
                        act.activation(x_hi[:, k, :], GU[k][:, :], ACT.Copy).then_inc(hi_done, 1)
                rounded(0)

                def step(n, o):
                    i = 2 * n + o
                    for j in range(SF + 1):
                        if j < SF:
                            c = SF * i + j
                            act.wait_ge(gu_done, 2 * c + 1)
                            at_least(act, gated_done, c)
                            act.activation(th, GU[2 * (j % 2)][:, :], ACT.Tanh, scale=0.5).then_inc(th_done, 1)
                        if j:
                            hid(i, j - 1)
                    if not last(i + 1):
                        rounded(i + 1)

                def hid(i, j):
                    c = SF * i + j
                    act.wait_ge(hidden_done, c + 1)
                    at_least(act, down_done, c - 1)
                    act.activation(hid_hi[:, j % 2, :], hidden, ACT.Copy).then_inc(hid_hi_done, 1)
                schedule(act, step)

            @block.vector
            def _(dve):
                def rest(i):
                    for k in range(KD):
                        dve.wait_ge(hi_done, KD * i + k + 1)
                        dve.tensor_tensor(x_lo[:, k, :], GU[k][:, :], x_hi[:, k, :].bitcast(F32),
                                          ALU.subtract).then_inc(x_done, 1)
                rest(0)

                def step(n, o):
                    i, q = 2 * n + o, o % 2
                    for j in range(SF):
                        c = SF * i + j
                        dve.wait_ge(th_done, c + 1)
                        at_least(dve, hid_done, c)
                        dve.scalar_tensor_tensor(hidden, th, 1.0, GU[2 * (j % 2)][:, :], ALU.add,
                                                 ALU.mult).then_inc(gated_done, 1)
                        dve.wait_ge(gated_done, c + 1)
                        dve.wait_ge(gu_done, 2 * c + 2)
                        dve.tensor_tensor(hidden, hidden, GU[2 * (j % 2) + 1][:, :],
                                          ALU.mult).then_inc(hidden_done, 1)
                        dve.wait_ge(hid_hi_done, c + 1)
                        dve.tensor_tensor(hid_lo[:, j % 2, :], hidden, hid_hi[:, j % 2, :].bitcast(F32),
                                          ALU.subtract).then_inc(hid_done, 1)
                    if not last(i + 1):
                        rest(i + 1)
                    dve.wait_ge(h_in[q], 16 * (n + o // 2) + 16)
                    dve.wait_ge(y_in, 16 * TOP * TT * (i + 1))
                    dve.wait_ge(down_done, SF * i + SF)

                    def col(ap, a):
                        j = TT * i + a
                        return ap[:, j:j + 1] if isinstance(i, int) else ap[:, bass.ds(j, 1)]
                    for a in range(TT):
                        dve.scalar_tensor_tensor(h[:, q, a, :], OUT[a][:, :], col(shared_gate, a), h[:, q, a, :],
                                                 ALU.mult, ALU.add).then_inc(sum_done, 1)
                    for k in range(TOP):
                        for a in range(TT):
                            if k == 0:
                                dve.wait_ge(sum_done, TT * i + a + 1)
                            else:
                                dve.wait_ge(first_done, TT * i + a + 1)
                            dve.scalar_tensor_tensor(h[:, q, a, :], y_rows[:, k, a, :], col(weight[:, k, :], a),
                                                     h[:, q, a, :], ALU.mult,
                                                     ALU.add).then_inc(first_done if k == 0 else out_done, 1)
                schedule(dve, step)

    with whole:
        with ExitStack() as ctx:
            sb, ps, _ = maker(ctx)
            slot_token = sb("slot_token", [128, BLOCKS], U32)
            block_expert = sb("block_expert", [1, BLOCKS], I32)
            with ExitStack() as logits:
                LG = maker(logits)[1]("LG", [128, J, E + 1])
                with ExitStack() as part:
                    norm_and_logits(part, LG)
                with ExitStack() as part:
                    slots(part, slot_token, block_expert, LG)
            with ExitStack() as part:
                routed_experts(part, slot_token, block_expert)
        with ExitStack() as part:
            shared_expert(part)
def program(nc, t):
    B, S, D = t["out"].shape
    IH = t["edT"].shape[1] // 2
    E, TWO_I = t["egT"].shape[1:]
    scratch = nc.dram_tensor("h1_d", (B, S, D), F32, kind="Internal").ap()
    t["h1"] = scratch
    t["h1f"] = scratch.rearrange("b s d -> (b s) d")
    gate_up, down = D // 128 * E * TWO_I, E * 2 * D
    with nc.sbuf_tensor("region", [128, gate_up + down], F32) as region:
        eg_w = region[:, 0:gate_up].rearrange("p (k e f) -> p k e f", e=E, f=TWO_I)
        ed_w = region[0:IH, gate_up:].rearrange("p (e h d) -> p e h d", e=E, h=2)
        tokens_and_attention(nc, t, later=[
            (eg_w.rearrange("p k e f -> p k (e f)"), t["egT"].rearrange("(k p) e f -> p k (e f)", p=128)),
            (ed_w, t["edT"].rearrange("e (h p) d -> p e h d", p=IH))])
        t["out"] = t["out"].rearrange("b s d -> (b s) d")
        experts(nc, t, eg_w, ed_w, region)


def kernel(**inputs):
    import numpy as np
    import concourse.bacc as bacc
    from concourse.bass_utils import run_bass_kernel_spmd as run

    i = {k: np.asarray(v) for k, v in inputs.items()}
    tok = {k[7:]: v for k, v in i.items() if k.startswith("L0_tok_")}
    att = {k[8:]: v for k, v in i.items() if k.startswith("L0_attn_")}
    ffn = {k[7:]: v for k, v in i.items() if k.startswith("L0_ffn_")}
    x = i["x"].transpose(0, 2, 1)
    CI = tok["up_b"].shape[0]
    D, L = att["gamma"].shape[0], tok["conv_bs"].shape[0]

    def blocks(a):
        return a.reshape(-1, 128, a.shape[1]).transpose(1, 0, 2).reshape(128, -1)

    vectors = {k: tok[k].reshape(-1, 1) for k in ("up_b", "bn_gamma", "bn_beta", "bn_mean", "bn_var")}
    vectors.update(
        gate_b=tok["conv_bs"][:, :CI].T,
        lin_b=tok["conv_bs"][:, CI:].reshape(L // 2, 2, CI).transpose(1, 2, 0).reshape(2 * CI, L // 2),
        tok_b=np.pad(tok["out_b"], (0, 128 - tok["out_b"].size)).reshape(-1, 1),
        gamma=att["gamma"].reshape(D // 128, 128).T, beta=att["beta"].reshape(D // 128, 128).T,
        b1=att["b1"].reshape(-1, 1), b2=att["b2"].reshape(-1, 1), b3=att["b3"].reshape(-1, 1))
    columns, width = vector_columns(L, D // 128)
    packed = np.zeros((128, width), np.float32)
    for name, a in vectors.items():
        packed[:, columns[name]] = np.tile(a, (128 // a.shape[0], 1))

    conv = tok["conv_ws"].transpose(3, 2, 0, 1)
    conv_w = np.zeros((2 * CI, L, 3, 2 * CI), np.float32)
    for tap in range(conv.shape[0]):
        conv_w[CI * (tap % 2):CI * (tap % 2) + CI, :, tap // 2] = conv[tap]
    conv_w[CI:, :, 2, CI:] = np.eye(CI)[:, None]

    w3 = np.zeros((128, 34), np.float32)
    w3[:64, 2], w3[64:, 3] = att["W3"][0], att["W3"][0]

    up = tok["up_w"].transpose(0, 2, 1)
    laid = {
        "xT": np.concatenate([x, x[:2]]),
        "up_w": np.concatenate([up, up], axis=2),
        "vectors": packed,
        "conv_w": conv_w,
        "cond_w": np.concatenate([tok["cond_ws"].transpose(2, 0, 1).reshape(-1, L * CI), tok["cond_bs"].reshape(1, L * CI)]),
        "tok_w": tok["out_w"].T,
        "W1T": att["W1"].T,
        "W2T": att["W2"].T,
        "w3": w3,
        "WqkvT": att["Wqkv"].T,
        "bqkv": att["bqkv"],
        "wout": np.concatenate([att["Wout"].T, att["bout"].reshape(1, D)]),
        "gateT": np.concatenate([ffn["gate_w"], ffn["shared_expert_gate_w"]]).T,
        "sharedT": np.concatenate([blocks(ffn[k].T) for k in ("shared_gate_w", "shared_up_w", "shared_down_w")], axis=1),
        "egT": ffn["gate_up_proj"].transpose(2, 0, 1),
        "edT": ffn["down_proj"].transpose(0, 2, 1),
    }
    nc = bacc.Bacc("TRN2", target_bir_lowering=False, num_devices=1)
    arrays, t = {}, {}
    for name, a in laid.items():
        a = np.ascontiguousarray(a)
        arrays[f"in_{name}"] = a
        t[name] = nc.dram_tensor(f"in_{name}", a.shape, mybir.dt.from_np(a.dtype), kind="ExternalInput").ap()
    shape = (x.shape[0], tok["out_b"].shape[0], 2 * x.shape[2])
    t["out"] = nc.dram_tensor("out_0", shape, F32, kind="ExternalOutput").ap()
    program(nc, t)
    r = run(nc, [arrays], core_ids=[0])
    return r.results[0]["out_0"]
```
